# Optimizing a Trainium2 kernel written in Bass

```python
import numpy as np
import jax
import jax.numpy as jnp

def _softmax(x, axis=-1):
    return jax.nn.softmax(x, axis=axis)

def _gelu(x):
    return jax.nn.gelu(x, approximate=True)

def _silu(x):
    return jax.nn.silu(x)

def _sigmoid(x):
    return jax.nn.sigmoid(x)

def _layernorm(x, axis=-1, eps=1e-05):
    m = jnp.mean(x, axis=axis, keepdims=True)
    v = jnp.var(x, axis=axis, keepdims=True)
    return (x - m) / jnp.sqrt(v + eps)

def _scatter_add(tgt, idx, src, axis=0):
    return tgt.at[idx].add(src)

def _segment_sum(src, seg, n):
    return jax.ops.segment_sum(src, seg, n)
kernel_name = 'mk_prb_d1_jaxref_r8_4913ad'

def setup_inputs(seed: int=0):
    np.random.seed(seed)
    _w = jnp.asarray

    def _L0_attn_setup():
        import jax, jax.numpy as jnp
        import numpy as np

        def soft_clamp(x, lo, hi, sharpness):
            c = (hi + lo) / 2.0
            r = (hi - lo) / 2.0
            xn = (x - c) / (r + 1e-08)
            return jnp.tanh(xn * sharpness) / sharpness * r + c
        key = jax.random.key(seed)
        ks = jax.random.split(key, 7)
        B, L, D, N = (2, 256, 128, 16)
        x = jax.random.normal(ks[0], (B, L, D), dtype=jnp.float32)
        Wdt = jax.random.normal(ks[1], (D, D), dtype=jnp.float32) * 0.02
        bdt = jnp.full((D,), -2.0, dtype=jnp.float32)
        WB = jax.random.normal(ks[2], (N, D), dtype=jnp.float32) * (1.0 / np.sqrt(D))
        WC = jax.random.normal(ks[3], (N, D), dtype=jnp.float32) * (1.0 / np.sqrt(D))
        A_log = jax.random.normal(ks[4], (D, N), dtype=jnp.float32) * 0.1
        Dp = jnp.full((D,), 0.1, dtype=jnp.float32)
        return {'x': x, 'Wdt': Wdt, 'bdt': bdt, 'WB': WB, 'WC': WC, 'A_log': A_log, 'Dp': Dp}
    _L0_attn_in = _L0_attn_setup()

    def _L0_ffn_setup():
        import jax, jax.numpy as jnp
        import numpy as np
        H = 128
        E = 64
        K = 8
        G = 8
        TOPK_GROUP = 4
        I_MOE = 64
        I_SHARED = 256
        SCALE = 2.5

        def relu2(x):
            return jnp.square(jax.nn.relu(x))

        def _route(xf, router_w, correction_bias):
            T = xf.shape[0]
            logits = xf @ router_w.T
            scores = jax.nn.sigmoid(logits)
            sfc = scores + correction_bias[None, :]
            grp = sfc.reshape(T, G, E // G)
            top2, _ = jax.lax.top_k(grp, 2)
            group_scores = top2.sum(-1)
            _, gidx = jax.lax.top_k(group_scores, TOPK_GROUP)
            gmask = jnp.zeros((T, G), sfc.dtype).at[jnp.arange(T)[:, None], gidx].set(1.0)
            emask = jnp.repeat(gmask, E // G, axis=1)
            masked = jnp.where(emask > 0, sfc, 0.0)
            _, tidx = jax.lax.top_k(masked, K)
            tw = jnp.take_along_axis(scores, tidx, axis=1)
            tw = tw / (tw.sum(-1, keepdims=True) + 1e-20)
            return (tidx, tw * SCALE)
        key = jax.random.key(seed)
        ks = jax.random.split(key, 7)
        x = jax.random.normal(ks[0], (2, 128, H), dtype=jnp.float32)
        router_w = jax.random.normal(ks[1], (E, H), dtype=jnp.float32) * 0.02
        correction_bias = jax.random.normal(ks[2], (E,), dtype=jnp.float32) * 0.01
        up_w = jax.random.normal(ks[3], (E, H, I_MOE), dtype=jnp.float32) * 0.02
        down_w = jax.random.normal(ks[4], (E, I_MOE, H), dtype=jnp.float32) * 0.02
        shared_up_w = jax.random.normal(ks[5], (H, I_SHARED), dtype=jnp.float32) * 0.02
        shared_down_w = jax.random.normal(ks[6], (I_SHARED, H), dtype=jnp.float32) * 0.02
        return {'x': x, 'router_w': router_w, 'correction_bias': correction_bias, 'up_w': up_w, 'down_w': down_w, 'shared_up_w': shared_up_w, 'shared_down_w': shared_down_w}
    _L0_ffn_in = _L0_ffn_setup()
    _d = {'L0_attn_x': _L0_attn_in['x'], 'L0_attn_Wdt': _L0_attn_in['Wdt'], 'L0_attn_bdt': _L0_attn_in['bdt'], 'L0_attn_WB': _L0_attn_in['WB'], 'L0_attn_WC': _L0_attn_in['WC'], 'L0_attn_A_log': _L0_attn_in['A_log'], 'L0_attn_Dp': _L0_attn_in['Dp'], 'L0_ffn_router_w': _L0_ffn_in['router_w'], 'L0_ffn_correction_bias': _L0_ffn_in['correction_bias'], 'L0_ffn_up_w': _L0_ffn_in['up_w'], 'L0_ffn_down_w': _L0_ffn_in['down_w'], 'L0_ffn_shared_up_w': _L0_ffn_in['shared_up_w'], 'L0_ffn_shared_down_w': _L0_ffn_in['shared_down_w']}
    _x0 = _d['L0_attn_x']
    _d['L0_attn_x'] = jax.random.normal(jax.random.fold_in(jax.random.key(seed), 1), (2, 2048, 128), dtype=_x0.dtype)
    del _x0
    return _d

def reference(L0_attn_x, L0_attn_Wdt, L0_attn_bdt, L0_attn_WB, L0_attn_WC, L0_attn_A_log, L0_attn_Dp, L0_ffn_router_w, L0_ffn_correction_bias, L0_ffn_up_w, L0_ffn_down_w, L0_ffn_shared_up_w, L0_ffn_shared_down_w):

    def _L0_attn_ref(x, Wdt, bdt, WB, WC, A_log, Dp):
        import jax, jax.numpy as jnp
        import numpy as np

        def soft_clamp(x, lo, hi, sharpness):
            c = (hi + lo) / 2.0
            r = (hi - lo) / 2.0
            xn = (x - c) / (r + 1e-08)
            return jnp.tanh(xn * sharpness) / sharpness * r + c
        dt = soft_clamp(jax.nn.softplus(x @ Wdt.T + bdt), 0.001, 0.1, 0.5)
        B_param = x @ WB.T
        C_param = x @ WC.T
        A = -jnp.exp(soft_clamp(A_log, -5.0, 5.0, 0.5))
        dt_A = soft_clamp(dt[..., None] * A[None, None], -8.0, 8.0, 0.5)
        dA = jnp.exp(dt_A)
        dB = dt[..., None] * B_param[:, :, None, :]
        dA_t = jnp.moveaxis(dA, 1, 0)
        dB_t = jnp.moveaxis(dB, 1, 0)
        x_t = jnp.moveaxis(x, 1, 0)
        C_t = jnp.moveaxis(C_param, 1, 0)
        h0 = jnp.zeros(x.shape[:1] + (x.shape[2], A.shape[1]), dtype=jnp.float32)

        def step(h, inp):
            dAt, dBt, xt, Ct = inp
            h = dAt * h + dBt * xt[..., None]
            h_norm = jnp.sqrt(jnp.sum(h * h, axis=(1, 2), keepdims=True))
            scale = jnp.minimum(20.0 / (h_norm + 1e-08), 1.0)
            h = h * scale
            y = jnp.einsum('bdn,bn->bd', h, Ct) + Dp * xt
            return (h, y)
        _, ys = jax.lax.scan(step, h0, (dA_t, dB_t, x_t, C_t))
        return jnp.moveaxis(ys, 0, 1)

    def _L0_ffn_ref(x, router_w, correction_bias, up_w, down_w, shared_up_w, shared_down_w):
        import jax, jax.numpy as jnp
        import numpy as np
        H = 128
        E = 64
        K = 8
        G = 8
        TOPK_GROUP = 4
        I_MOE = 64
        I_SHARED = 256
        SCALE = 2.5

        def relu2(x):
            return jnp.square(jax.nn.relu(x))

        def _route(xf, router_w, correction_bias):
            T = xf.shape[0]
            logits = xf @ router_w.T
            scores = jax.nn.sigmoid(logits)
            sfc = scores + correction_bias[None, :]
            grp = sfc.reshape(T, G, E // G)
            top2, _ = jax.lax.top_k(grp, 2)
            group_scores = top2.sum(-1)
            _, gidx = jax.lax.top_k(group_scores, TOPK_GROUP)
            gmask = jnp.zeros((T, G), sfc.dtype).at[jnp.arange(T)[:, None], gidx].set(1.0)
            emask = jnp.repeat(gmask, E // G, axis=1)
            masked = jnp.where(emask > 0, sfc, 0.0)
            _, tidx = jax.lax.top_k(masked, K)
            tw = jnp.take_along_axis(scores, tidx, axis=1)
            tw = tw / (tw.sum(-1, keepdims=True) + 1e-20)
            return (tidx, tw * SCALE)
        B, S, Hd = x.shape
        xf = x.reshape(-1, Hd)
        T = xf.shape[0]
        tidx, tw = _route(xf.astype(jnp.float32), router_w, correction_bias)
        combine = jnp.zeros((T, E), xf.dtype).at[jnp.arange(T)[:, None], tidx].add(tw.astype(xf.dtype))

        def body(acc, ew):
            wu, wd, c = ew
            return (acc + c[:, None] * (relu2(xf @ wu) @ wd), None)
        routed, _ = jax.lax.scan(body, jnp.zeros_like(xf), (up_w, down_w, combine.T))
        shared = relu2(xf @ shared_up_w) @ shared_down_w
        return (routed + shared).reshape(B, S, Hd)
    x = L0_attn_x
    xn = _layernorm(x, axis=-1)
    x = x + _L0_attn_ref(xn, L0_attn_Wdt, L0_attn_bdt, L0_attn_WB, L0_attn_WC, L0_attn_A_log, L0_attn_Dp) + _L0_ffn_ref(xn, L0_ffn_router_w, L0_ffn_correction_bias, L0_ffn_up_w, L0_ffn_down_w, L0_ffn_shared_up_w, L0_ffn_shared_down_w)
    return x

_drawn_inputs = setup_inputs


def setup_inputs(seed=0):
    import zlib

    import numpy as np

    out = dict(_drawn_inputs(seed))
    spreads = {'L0_attn_bdt': (-2.0, 0.2), 'L0_attn_Dp': (0.10000000149011612, 0.6)}
    factors = {'L0_ffn_router_w': 8.0,
     'L0_ffn_correction_bias': 8.0,
     'L0_ffn_up_w': 8.0,
     'L0_ffn_down_w': 8.0,
     'L0_ffn_shared_up_w': 4.821,
     'L0_ffn_shared_down_w': 4.444,
     'L0_attn_A_log': 4.056}
    for name, (base, spread) in spreads.items():
        noise = np.random.default_rng([zlib.crc32(name.encode()), seed]).standard_normal(out[name].shape)
        drawn = base * np.exp(spread * noise) if base else spread * noise
        out[name] = jnp.asarray(drawn.astype(out[name].dtype))
    for name, factor in factors.items():
        out[name] = (out[name] * factor).astype(out[name].dtype)
    return out
```

```python
from contextlib import ExitStack

import numpy as np

import concourse.bass as bass
from concourse import mybir

F32 = mybir.dt.float32
F32R = mybir.dt.float32r
BF16 = mybir.dt.bfloat16
I32 = mybir.dt.int32
ALU = mybir.AluOpType
ACT = mybir.ActivationFunctionType
AX = mybir.AxisListType

P = 128
LOG1P = [0.999999970540657, -0.49999501516787703, 0.33319271342517287, -0.24844369892616386,
         0.19111431081225275, -0.13674769707020493, 0.07836166803754308, -0.029588507405152252,
         0.005253457800249444]
NORM_LIMIT = 20.0
SAFE_SQUARE = NORM_LIMIT * NORM_LIMIT * 0.99
DT_MID, DT_HALF = (0.1 + 0.001) / 2, (0.1 - 0.001) / 2


def layer_program(nc, x_in, wdt_in, bdt_in, wb_in, wc_in, alog_in, dp_in, rw_in, cbias_in,
                  up_in, down_in, sup_in, sdown_in, out):
    BATCH, SEQ, D = x_in.shape
    N = wb_in.shape[0]
    E, _, I = up_in.shape
    SH = sup_in.shape[1]
    T = BATCH * SEQ
    CT = 512
    NCH = T // CT
    CPB = SEQ // CT
    KB = CT // P
    PAIRS = E // 2
    SHP = SH // P
    SLOTS = PAIRS + SHP
    G, TOPG = 8, 4
    EG = E // G
    RSTEPS = 11

    x_flat = x_in.rearrange("b l d -> (b l) d")
    out_flat = out.rearrange("b l d -> (b l) d")

    def x_chunk(c):
        return x_flat[bass.ds(c * CT, CT), :].rearrange("(k p) d -> p k d", p=P)

    def out_chunk(c):
        return out_flat[bass.ds(c * CT, CT), :].rearrange("(k p) d -> p k d", p=P)

    def col(v):
        return v.rearrange("(p a) -> p a", a=1)

    with ExitStack() as ctx:
        def sb(name, shape, dt=F32):
            return ctx.enter_context(nc.sbuf_tensor(name, shape, dt))

        def sem(name):
            return ctx.enter_context(nc.semaphore(name))

        up_hi, up_lo = sb("up_hi", [P, E * I], F32R), sb("up_lo", [P, E * I], F32R)
        down = sb("down", [P, PAIRS, D])
        sup_hi, sup_lo = sb("sup_hi", [P, SH], F32R), sb("sup_lo", [P, SH], F32R)
        sdown = sb("sdown", [P, SHP, D])
        proj_hi, proj_lo = sb("proj_hi", [P, 3, P], F32R), sb("proj_lo", [P, 3, P], F32R)
        onehot_e = sb("onehot_e", [P, E, I], F32R)
        onehot_bc = sb("onehot_bc", [P, 2 * N], F32R)
        ident = sb("ident", [P, P])
        a16 = sb("a16", [P, N])
        dtbias = sb("dtbias", [P, 1])
        bdt, dp = sb("bdt", [P, 1]), sb("dp", [P, 1])
        keep = sb("keep", [P, NCH])
        cbias = sb("cbias", [P, E])
        before = sb("before", [P, G, G])
        halves = sb("halves", [P, KB])
        dt_all, dtx_all, rest = sb("dt_all", [P, T]), sb("dtx_all", [P, T]), sb("rest", [P, T])
        bc_all = sb("bc_all", [P, T], F32R)

        x_hi, x_lo = sb("x_hi", [P, 2 * CT], F32R), sb("x_lo", [P, 2 * CT], F32R)
        comb = sb("comb", [P, 2 * CT], F32R)

        xs, xn = sb("xs", [P, KB, D]), sb("xn", [P, KB, D])
        stats, mv = sb("stats", [P, KB, 6]), sb("mv", [P, KB, 2])
        vare, rstd = sb("vare", [P, KB]), sb("rstd", [P, KB])
        xt = sb("xt", [P, CT])
        zt, wexp, poly, zpos = sb("zt", [P, CT]), sb("wexp", [P, CT]), sb("poly", [P, CT]), sb("zpos", [P, CT])
        logit = xn[:, :, :].rearrange("p k d -> p (k d)")
        sig, sfc = sb("sig", [P, KB, E]), sb("sfc", [P, KB, E])
        t4a, t4b = sb("t4a", [P, KB * G, 4]), sb("t4b", [P, KB * G, 4])
        t2a, t2b, t2c = sb("t2a", [P, KB * G, 2]), sb("t2b", [P, KB * G, 2]), sb("t2c", [P, KB * G, 2])
        g1a, g1b, g1c = sb("g1a", [P, KB * G]), sb("g1b", [P, KB * G]), sb("g1c", [P, KB * G])
        cmp_a, cmp_b = sb("cmp_a", [P, KB * G, G]), sb("cmp_b", [P, KB * G, G])
        top8 = sb("top8", [P, KB, 8])
        masked, picked = sb("masked", [P, KB, E]), sb("picked", [P, KB, E])
        wsum, wrec = sb("wsum", [P, KB]), sb("wrec", [P, KB])
        cc = sb("cc", [P, KB, 2, E])

        relu, sq, act = sb("relu", [P, 2, CT]), sb("sq", [P, 2, CT]), sb("act", [P, 2, CT])
        decay, db = sb("decay", [P, 2, CT]), sb("db", [P, CT])
        h = sb("h", [P, 2, CT])
        carry = sb("carry", [P, N])
        prod, yacc = sb("prod", [P, 2, CT]), sb("yacc", [P, CT])
        ot, xr, res = sb("ot", [P, CT]), sb("xr", [P, KB, D]), sb("res", [P, KB, D])
        gmax = sb("gmax", [P, NCH])
        gm1, gmt, flag = sb("gm1", [P, 1]), sb("gmt", [1, 1]), sb("flag", [1, 1], I32)
        colb = sb("colb", [P, 2, P], F32R)
        ones = relu[:, 0, 0:P]
        bcs, hs, da = (relu[:, 1, o:o + 2 * w].rearrange("p (b n) -> p b n", b=2)
                       for o, w in ((0, 2 * N), (128, N), (192, N)))
        junk, ss, nrm, scl = sb("junk", [P, 2, N]), sb("ss", [P, 2]), sb("nrm", [P, 2]), sb("scl", [P, 2])

        up_raw = rest
        small = dt_all[:, 0:3 * P].rearrange("p (a k) -> p a k", a=3)
        sup_raw = dt_all[:, 3 * P:3 * P + SH]
        alog = dt_all[:, 1024:1024 + N]
        th = dt_all[:, 1088:1088 + N]
        ea = dt_all[:, 1152:1152 + N]
        ident_r = dtx_all[:, 0:P]
        oh64 = dtx_all[:, P:P + E]
        smallt = dtx_all[:, 512:512 + 3 * P]

        def bank(name):
            return ctx.enter_context(nc.psum_tensor(name, [P, CT], F32))

        U = [bank("U0"), bank("U1")]
        CB = bank("CB")
        DN = bank("DN")
        BB, BCC = bank("BB"), bank("BCC")
        GR = bank("GR")
        M = bank("M")

        w_small, w_up, w_down, w_late = sem("w_small"), sem("w_up"), sem("w_down"), sem("w_late")
        const_ready, pool_init = sem("const_ready"), sem("pool_init")
        wt_ready, proj_ready, up_split, act_init, dve_init = (
            sem("wt_ready"), sem("proj_ready"), sem("up_split"), sem("act_init"), sem("dve_init"))
        x_loaded, xr_loaded, stored = sem("x_loaded"), sem("xr_loaded"), sem("stored")
        dve_prep, pool_prep, act_prep = sem("dve_prep"), sem("pool_prep"), sem("act_prep")
        var_ready, rstd_ready, xn_ready = sem("var_ready"), sem("rstd_ready"), sem("xn_ready")
        xt_done, xhi_ready, xlo_ready = sem("xt_done"), sem("xhi_ready"), sem("xlo_ready")
        z_done, z_copied, wexp_ready, sp_ready, th_ready, dt_ready, dtx_ready = (
            sem("z_done"), sem("z_copied"), sem("wexp_ready"), sem("sp_ready"), sem("th_ready"),
            sem("dt_ready"), sem("dtx_ready"))
        bc_done, bchi_ready, bclo_ready = sem("bc_done"), sem("bchi_ready"), sem("bclo_ready")
        lg_done, lg_copied, lgt_done, sig_exp = sem("lg_done"), sem("lg_copied"), sem("lgt_done"), sem("sig_exp")
        cc_ready, ct_done, chi_ready, clo_ready = sem("cc_ready"), sem("ct_done"), sem("chi_ready"), sem("clo_ready")
        up_done, relu_done, sq_done, cb_done, mul_done, down_done = (
            sem("up_done"), sem("relu_done"), sem("sq_done"), sem("cb_done"), sem("mul_done"), sem("down_done"))
        tanh_done, exp_done, bb_done, bcc_done, db_done, scan_done = (
            sem("tanh_done"), sem("exp_done"), sem("bb_done"), sem("bcc_done"), sem("db_done"), sem("scan_done"))
        ym_done, yacc_done, carry_done, gram_done = (
            sem("ym_done"), sem("yacc_done"), sem("carry_done"), sem("gram_done"))
        rest_done, ot_ready, ot_done, res_ready, diag_done, gmax_done = (
            sem("rest_done"), sem("ot_ready"), sem("ot_done"), sem("res_ready"), sem("diag_done"), sem("gmax_done"))
        g_end, flag_ready = sem("g_end"), sem("flag_ready")
        passed = sem("passed")
        s_step_dve = sem("s_step_dve")
        s_col, s_bc, s_exp, s_ss, s_norm, s_sqrt, s_ot, s_otd, s_res, s_store, s_xr = (
            sem("s_col"), sem("s_bc"), sem("s_exp"), sem("s_ss"), sem("s_norm"),
            sem("s_sqrt"), sem("s_ot"), sem("s_otd"), sem("s_res"), sem("s_store"), sem("s_xr"))

        def wait(eng, s, value):
            if not isinstance(value, int) or value > 0:
                eng.wait_ge(s, value)

        def alone(eng):
            eng.sem_inc(passed, 1)

        def sl(c):
            return bass.ds(c * CT, CT)

        def par(c):
            return bass.ds((c % 2) * CT, CT)

        DVE_PREP = 23 + 2 * KB
        POOL_PREP = 18
        ACT_PREP = 1

        class Chain:

            def __init__(self, eng, s, base):
                self.eng, self.s, self.base, self.n = eng, s, base, 0

            def then(self, ins):
                ins.then_inc(self.s, 1)
                self.n += 1

            def wait(self, by_itself=False):
                wait(self.eng, self.s, self.base + self.n)
                if by_itself:
                    alone(self.eng)

        block = ctx.enter_context(nc.Block())

        @block.sync
        def _(sp):
            for r in range(P // (2 * N)):
                sp.dma_start(small[2 * N * r:2 * N * r + N, 1, :], wb_in).then_inc(w_small, 16)
                sp.dma_start(small[2 * N * r + N:2 * N * (r + 1), 1, :], wc_in).then_inc(w_small, 16)
            sp.dma_start(small[:, 0, :], wdt_in).then_inc(w_small, 16)
            for r in range(P // E):
                sp.dma_start(small[E * r:E * (r + 1), 2, :], rw_in).then_inc(w_small, 16)
            sp.dma_start(xs[:, :, :], x_chunk(0)).then_inc(x_loaded, 16)
            sp.dma_start(alog, alog_in).then_inc(w_late, 16)
            sp.dma_start(bdt[:, :], col(bdt_in)).then_inc(w_late, 16)
            sp.dma_start(dp[:, :], col(dp_in)).then_inc(w_late, 16)
            sp.dma_start(cbias[:, :], cbias_in.rearrange("(a e) -> a e", a=1).broadcast_to([P, E])).then_inc(w_late, 16)
            sp.dma_start(sup_raw, sup_in).then_inc(w_late, 16)
            for q in range(4):
                e0, e1 = q * E // 4, (q + 1) * E // 4
                sp.dma_start(up_raw[:, e0 * I:e1 * I].rearrange("p (e i) -> p e i", i=I),
                             up_in[e0:e1].rearrange("e h i -> h e i")).then_inc(w_up, 16)
            sp.dma_start(down[:, :, :], down_in.rearrange("(j e) i h -> (e i) j h", e=2)).then_inc(w_down, 16)
            sp.dma_start(sdown[:, :, :], sdown_in.rearrange("(j p) h -> p j h", p=P)).then_inc(w_down, 16)

            def transfers(c, first, last):
                if not last:
                    wait(sp, xn_ready, c + 1)
                    alone(sp)
                    sp.dma_start(xs[:, :, :], x_chunk(c + 1)).then_inc(x_loaded, 16)
                if not first:
                    sp.dma_start(xr[:, :, :], x_chunk(c - 1)).then_inc(xr_loaded, 16)
                    wait(sp, res_ready, c)
                    alone(sp)
                    sp.dma_start(out_chunk(c - 1), res[:, :, :]).then_inc(stored, 16)
                    sp.wait_ge(stored, 16 * c)
                    alone(sp)

            transfers(0, True, False)
            with sp.Fori(1, NCH - 1) as c:
                transfers(c, False, False)
            transfers(NCH - 1, False, True)
            transfers(NCH, False, True)
            sp.wait_ge(flag_ready, 1)
            safe = sp.value_load(flag[0:1, 0:1])
            with sp.If(safe == 0):
                with sp.Fori(0, NCH) as c:
                    sp.dma_start(xr[:, :, :], x_chunk(c)).then_inc(s_xr, 16)
                    sp.wait_ge(s_res, c + 1)
                    alone(sp)
                    sp.dma_start(out_chunk(c), res[:, :, :]).then_inc(s_store, 16)
                    sp.wait_ge(s_store, 16 * (c + 1))
                    alone(sp)

        @block.gpsimd
        def _(pool):
            g = nc.gpsimd
            n_init = [0]

            def init(ins):
                ins.then_inc(pool_init, 1)
                n_init[0] += 1
                pool.wait_ge(pool_init, n_init[0])

            init(g.memset(ident[:, :], 0.0))
            init(g.affine_select(out=ident[:, :], in_=ident[:, :], compare_op=ALU.not_equal, fill=1.0,
                                 base=0, pattern=[[-1, P]], channel_multiplier=1))
            init(g.memset(oh64, 0.0))
            for base in (0, -E):
                init(g.affine_select(out=oh64, in_=oh64, compare_op=ALU.not_equal, fill=1.0,
                                     base=base, pattern=[[-1, E]], channel_multiplier=1))
            init(g.memset(before[:, :, :], 1.0))
            init(g.affine_select(out=before[:, :, :], in_=before[:, :, :], compare_op=ALU.is_gt, fill=0.0,
                                 base=0, pattern=[[1, G], [-1, G]], channel_multiplier=0))
            init(g.memset(halves[:, :], -0.5))
            init(g.memset(keep[:, :], 1.0))
            for b in range(BATCH):
                init(g.memset(keep[:, b * CPB:b * CPB + 1], 0.0))
            init(g.memset(carry[:, :], 0.0))
            g.memset(gmt[:, :], 0.0).then_inc(const_ready, 1)

            def prep(pc, slot):
                chain = chains["p"]
                if slot == 2:
                    pool.wait_ge(var_ready, pc + 1)
                    alone(pool)
                    chain.then(g.tensor_scalar(vare[:, :], mv[:, :, 1], 1e-5, None, ALU.add))
                    chain.wait(True)
                    g.tensor_tensor(rstd[:, :], vare[:, :], halves[:, :], ALU.pow).then_inc(rstd_ready, 1)
                if slot == 8:
                    pool.wait_ge(xlo_ready, pc + 1)
                    pool.wait_ge(xhi_ready, pc + 1)
                    alone(pool)
                    chain.then(g.tensor_tensor(xt[:, :], x_hi[:, par(pc)].bitcast(F32),
                                               x_lo[:, par(pc)].bitcast(F32), ALU.add))
                if slot == 11:
                    pool.wait_ge(wexp_ready, pc + 1)
                    alone(pool)
                    chain.then(g.tensor_scalar(poly[:, :], wexp[:, :], LOG1P[-1], LOG1P[-2], ALU.mult, ALU.add))
                if 12 <= slot < 12 + len(LOG1P) - 2:
                    k = len(LOG1P) - 3 - (slot - 12)
                    chain.wait(True)
                    chain.then(g.tensor_tensor(poly[:, :], poly[:, :], wexp[:, :], ALU.mult))
                    chain.wait(True)
                    chain.then(g.tensor_scalar(poly[:, :], poly[:, :], LOG1P[k], None, ALU.add))
                if slot == 19:
                    chain.wait(True)
                    chain.then(g.tensor_tensor(poly[:, :], poly[:, :], wexp[:, :], ALU.mult))
                    chain.wait(True)
                    g.tensor_tensor(poly[:, :], poly[:, :], zpos[:, :], ALU.add).then_inc(sp_ready, 1)
                if slot == 23:
                    pool.wait_ge(dt_ready, pc + 1)
                    alone(pool)
                    if isinstance(pc, int) and pc == 0:
                        pool.wait_ge(up_split, 2)
                    g.tensor_tensor(rest[:, sl(pc)], xt[:, :], dp[:, 0:1].broadcast_to([P, CT]), ALU.mult)
                    g.tensor_tensor(dtx_all[:, sl(pc)], dt_all[:, sl(pc)], xt[:, :], ALU.mult).then_inc(dtx_ready, 1)

            def main(c, slot):
                if slot % 2 == 0 and 2 <= slot <= 2 * N:
                    n = slot // 2 - 1
                    pool.wait_ge(scan_done, c * N + n + 1)
                    alone(pool)
                    nxt = NCH - 1 if isinstance(c, int) and c == NCH - 1 else c + 1
                    g.tensor_tensor(carry[:, n:n + 1], h[:, n % 2, CT - 1:CT], keep[:, bass.ds(nxt, 1)],
                                    ALU.mult).then_inc(carry_done, 1)
                    if n:
                        pool.wait_ge(ym_done, c * N + n + 1)
                        wait(pool, yacc_done, c * (N - 1) + n - 1)
                        g.tensor_tensor(yacc[:, :], yacc[:, :], prod[:, n % 2, :], ALU.add).then_inc(yacc_done, 1)

            chains = {}

            def chunk(c, last):
                if not last:
                    chains["p"] = Chain(pool, pool_prep, (c + 1) * POOL_PREP)
                for slot in range(SLOTS):
                    main(c, slot)
                    if not last:
                        prep(c + 1, slot)
                assert last or chains["p"].n == POOL_PREP, chains["p"].n

            chains["p"] = Chain(pool, pool_prep, 0)
            pool.wait_ge(w_late, 5 * 16)
            pool.wait_ge(act_init, 3)
            for slot in range(SLOTS):
                prep(0, slot)
            chunk(0, False)
            with pool.Fori(1, NCH - 1) as c:
                chunk(c, False)
            chunk(NCH - 1, True)

        @block.scalar
        def _(act_e):
            a = nc.scalar
            act_e.wait_ge(w_late, 5 * 16)
            a.activation(th, alog, ACT.Tanh, scale=0.1).then_inc(act_init, 1)
            act_e.wait_ge(act_init, 1)
            a.activation(ea, th, ACT.Exp, scale=10.0).then_inc(act_init, 1)
            a.activation(sup_hi[:, :], sup_raw, ACT.Copy).then_inc(act_init, 1)
            act_e.wait_ge(wt_ready, 3)
            a.activation(proj_hi[:, :, :].rearrange("p a k -> p (a k)"), M[:, 0:3 * P], ACT.Copy).then_inc(proj_ready, 1)

            def prep(pc, slot):
                if slot == 6:
                    act_e.wait_ge(xt_done, pc + 1)
                    alone(act_e)
                    a.activation(x_hi[:, par(pc)], M[:, :], ACT.Copy).then_inc(xhi_ready, 1)
                if slot == 9:
                    act_e.wait_ge(z_done, pc + 1)
                    wait(act_e, sp_ready, pc)
                    a.activation(zt[:, :], M[:, :], ACT.Identity, bias=bdt[:, 0:1]).then_inc(z_copied, 1)
                    act_e.wait_ge(z_copied, pc + 1)
                    a.activation(zpos[:, :], zt[:, :], ACT.Relu)
                    a.activation(wexp[:, :], zt[:, :], ACT.Abs).then_inc(act_prep, 1)
                if slot == 10:
                    act_e.wait_ge(act_prep, pc + 1)
                    a.activation(wexp[:, :], wexp[:, :], ACT.Exp, scale=-1.0).then_inc(wexp_ready, 1)
                if slot == 11:
                    act_e.wait_ge(bc_done, pc + 1)
                    alone(act_e)
                    a.activation(bc_all[:, sl(pc)], M[:, :], ACT.Copy).then_inc(bchi_ready, 1)
                if slot == 14:
                    act_e.wait_ge(lg_done, pc + 1)
                    a.activation(logit[:, :], M[:, :], ACT.Copy).then_inc(lg_copied, 1)
                if slot == 16:
                    act_e.wait_ge(lgt_done, pc + 1)
                    a.activation(sig[:, :, :].rearrange("p k e -> p (k e)"), M[:, 0:KB * E], ACT.Exp,
                                 scale=-1.0).then_inc(sig_exp, 1)
                if slot == 21:
                    act_e.wait_ge(sp_ready, pc + 1)
                    a.activation(zt[:, :], poly[:, :], ACT.Tanh, scale=0.5 / DT_HALF,
                                 bias=dtbias[:, 0:1]).then_inc(th_ready, 1)
                if slot == 31:
                    act_e.wait_ge(ct_done, pc + 1)
                    alone(act_e)
                    a.activation(comb[:, par(pc)], M[:, :], ACT.Copy).then_inc(chi_ready, 1)

            def main(c, slot):
                s = c * SLOTS + slot
                n = slot // 2
                act_e.wait_ge(up_done, s + 1)
                wait(act_e, sq_done, s - 1)
                a.activation(relu[:, slot % 2, :], U[slot % 2][:, :], ACT.Relu).then_inc(relu_done, 1)
                if n < N and slot % 2 == 0:
                    wait(act_e, scan_done, c * N + n - 1)
                    alone(act_e)
                    a.activation(decay[:, n % 2, :], dt_all[:, sl(c)], ACT.Tanh, scale=a16[:, n:n + 1]).then_inc(tanh_done, 1)
                if n < N and slot % 2 == 1:
                    act_e.wait_ge(tanh_done, c * N + n + 1)
                    a.activation(decay[:, n % 2, :], decay[:, n % 2, :], ACT.Exp, scale=16.0).then_inc(exp_done, 1)
                act_e.wait_ge(relu_done, s + 1)
                if slot < PAIRS:
                    wait(act_e, mul_done, c * PAIRS + slot - 1)
                    a.activation(sq[:, slot % 2, :], relu[:, slot % 2, :], ACT.Square).then_inc(sq_done, 1)
                else:
                    wait(act_e, down_done, s - 1)
                    a.activation(act[:, slot % 2, :], relu[:, slot % 2, :], ACT.Square).then_inc(sq_done, 1)

            def chunk(c, last):
                for slot in range(SLOTS):
                    if slot == 0:
                        act_e.wait_ge(dt_ready, c + 1)
                    main(c, slot)
                    if not last:
                        prep(c + 1, slot)

            act_e.wait_ge(dve_init, 2)
            for slot in range(SLOTS):
                if slot == 17:
                    act_e.wait_ge(w_up, 16 * 4)
                    a.activation(up_hi[:, :], up_raw[:, :], ACT.Copy).then_inc(up_split, 1)
                prep(0, slot)
            chunk(0, False)
            with act_e.Fori(1, NCH - 1) as c:
                chunk(c, False)
            chunk(NCH - 1, True)

            act_e.wait_ge(flag_ready, 1)
            safe = act_e.value_load(flag[0:1, 0:1])
            with act_e.If(safe == 0):
                with act_e.Fori(0, SEQ) as t:
                    for b in range(2):
                        i = a.activation(da[:, b, :], a16[:, :], ACT.Tanh, scale=dt_all[:, bass.ds(t + b * SEQ, 1)])
                    i.then_inc(s_exp, 1)
                    act_e.wait_ge(s_exp, 2 * t + 1)
                    a.activation(da[:, :, :], da[:, :, :], ACT.Exp, scale=16.0).then_inc(s_exp, 1)
                    act_e.wait_ge(s_norm, t + 1)
                    a.activation(nrm[:, :], M[:, 64:66], ACT.Sqrt).then_inc(s_sqrt, 1)

        @block.vector
        def _(dve):
            v = nc.vector
            dve.wait_ge(act_init, 3)
            v.tensor_scalar(a16[:, :], ea, -1.0 / 16, None, ALU.mult).then_inc(dve_init, 1)
            v.memset(dtbias[:, :], -0.5 * DT_MID / DT_HALF).then_inc(dve_init, 1)
            v.tensor_tensor(sup_lo[:, :], sup_raw, sup_hi[:, :].bitcast(F32), ALU.subtract)
            dve.wait_ge(const_ready, 1)
            v.tensor_copy(onehot_bc[:, :], oh64[:, 0:2 * N])
            v.tensor_copy(onehot_e[:, :, :], oh64.unsqueeze(2).broadcast_to([P, E, I])).then_inc(dve_init, 1)
            dve.wait_ge(proj_ready, 1)
            v.tensor_tensor(proj_lo[:, :, :].rearrange("p a k -> p (a k)"), M[:, 0:3 * P],
                            proj_hi[:, :, :].rearrange("p a k -> p (a k)").bitcast(F32), ALU.subtract).then_inc(proj_ready, 1)

            def dup(t, n):
                return t.unsqueeze(2).broadcast_to([P, KB * G, n])

            sfc_g = sfc[:, :, :].rearrange("p k (g e) -> p (k g) e", g=G)
            gs3 = g1a[:, :].rearrange("p (k g) -> p k g", g=G)
            c3 = cmp_a[:, :, :].rearrange("p (k g) h -> p k g h", g=G)
            d3 = cmp_b[:, :, :].rearrange("p (k g) h -> p k g h", g=G)

            def gs_h():
                return gs3.unsqueeze(2).broadcast_to([P, KB, G, G])

            def gs_g():
                return gs3.unsqueeze(3).broadcast_to([P, KB, G, G])

            def prep(pc, slot):
                ch = chains["v"]

                def op(f, *args, **kw):
                    ch.wait(f in (v.max, v.match_replace))
                    ch.then(f(*args, **kw))

                if slot == 1:
                    dve.wait_ge(x_loaded, 16 * (pc + 1))
                    for k in range(KB):
                        i = v.bn_stats(stats[:, k, :], xs[:, k, :])
                    ch.then(i)
                    ch.wait(True)
                    for k in range(KB):
                        i = v.bn_aggr(mv[:, k, :], stats[:, k, :])
                    i.then_inc(var_ready, 1)
                if slot == 3:
                    dve.wait_ge(rstd_ready, pc + 1)
                    wait(dve, lgt_done, pc)
                    for k in range(KB):
                        i = v.tensor_scalar(xn[:, k, :], xs[:, k, :], mv[:, k, 0:1], rstd[:, k:k + 1],
                                            ALU.subtract, ALU.mult)
                    i.then_inc(xn_ready, 1)
                if slot == 7:
                    dve.wait_ge(xhi_ready, pc + 1)
                    v.tensor_tensor(x_lo[:, par(pc)], M[:, :], x_hi[:, par(pc)].bitcast(F32),
                                    ALU.subtract).then_inc(xlo_ready, 1)
                if slot == 12:
                    dve.wait_ge(bchi_ready, pc + 1)
                    v.tensor_tensor(bc_all[E:P, sl(pc)], M[E:P, :], bc_all[E:P, sl(pc)].bitcast(F32),
                                    ALU.subtract).then_inc(bclo_ready, 1)
                if slot == 17:
                    dve.wait_ge(sig_exp, pc + 1)
                    ch.then(v.tensor_scalar(sig[:, :, :], sig[:, :, :], 1.0, None, ALU.add))
                    op(v.reciprocal, sig[:, :, :], sig[:, :, :])
                    op(v.tensor_tensor, sfc[:, :, :], sig[:, :, :],
                       cbias[:, :].unsqueeze(1).broadcast_to([P, KB, E]), ALU.add)
                if slot == 18:
                    ch.wait()
                    v.tensor_tensor(t4a[:, :, :], sfc_g[:, :, 0:4], sfc_g[:, :, 4:8], ALU.max)
                    ch.then(v.tensor_tensor(t4b[:, :, :], sfc_g[:, :, 0:4], sfc_g[:, :, 4:8], ALU.min))
                    ch.wait()
                    v.tensor_tensor(t2a[:, :, :], t4a[:, :, 0:2], t4a[:, :, 2:4], ALU.max)
                    v.tensor_tensor(t2b[:, :, :], t4a[:, :, 0:2], t4a[:, :, 2:4], ALU.min)
                    ch.then(v.tensor_tensor(t2c[:, :, :], t4b[:, :, 0:2], t4b[:, :, 2:4], ALU.max))
                    op(v.tensor_tensor, t2b[:, :, :], t2b[:, :, :], t2c[:, :, :], ALU.max)
                if slot == 19:
                    ch.wait()
                    v.tensor_tensor(g1a[:, :], t2a[:, :, 0], t2a[:, :, 1], ALU.max)
                    v.tensor_tensor(g1b[:, :], t2a[:, :, 0], t2a[:, :, 1], ALU.min)
                    ch.then(v.tensor_tensor(g1c[:, :], t2b[:, :, 0], t2b[:, :, 1], ALU.max))
                    op(v.tensor_tensor, g1b[:, :], g1b[:, :], g1c[:, :], ALU.max)
                    op(v.tensor_tensor, g1a[:, :], g1a[:, :], g1b[:, :], ALU.add)
                if slot == 20:
                    ch.wait()
                    v.tensor_tensor(c3, gs_h(), gs_g(), ALU.is_gt)
                    ch.then(v.tensor_tensor(d3, gs_h(), gs_g(), ALU.is_equal))
                    op(v.tensor_tensor, d3, d3, before[:, :, :].unsqueeze(1).broadcast_to([P, KB, G, G]), ALU.mult)
                    op(v.tensor_tensor, cmp_a[:, :, :], cmp_a[:, :, :], cmp_b[:, :, :], ALU.add)
                if slot == 21:
                    op(v.tensor_reduce, g1b[:, :], cmp_a[:, :, :], axis=AX.X, op=ALU.add)
                    op(v.tensor_scalar, g1c[:, :], g1b[:, :], TOPG - 0.5, None, ALU.is_lt)
                    op(v.tensor_tensor, masked[:, :, :].rearrange("p k (g e) -> p (k g) e", g=G), sfc_g,
                       dup(g1c[:, :], EG), ALU.mult)
                    op(v.tensor_scalar, masked[:, :, :], masked[:, :, :], 0.0, None, ALU.add)
                if 22 <= slot < 22 + KB:
                    k = slot - 22
                    op(v.max, top8[:, k, :], masked[:, k, :])
                    op(v.match_replace, out=picked[:, k, :], in_to_replace=top8[:, k, :], in_values=masked[:, k, :],
                       imm_value=-3.0e38)
                if slot == 26:
                    op(v.tensor_tensor, picked[:, :, :], picked[:, :, :], masked[:, :, :], ALU.not_equal)
                    op(v.tensor_tensor, picked[:, :, :], picked[:, :, :], sig[:, :, :], ALU.mult)
                    op(v.tensor_reduce, wsum[:, :], picked[:, :, :], axis=AX.X, op=ALU.add)
                if slot == 27:
                    op(v.tensor_scalar, wsum[:, :], wsum[:, :], 1e-20, None, ALU.add)
                    op(v.reciprocal, wrec[:, :], wsum[:, :])
                    op(v.tensor_scalar, wrec[:, :], wrec[:, :], 2.5, None, ALU.mult)
                if slot == 28:
                    ch.wait()
                    wait(dve, ct_done, pc)
                    for r in range(2):
                        i = v.tensor_tensor(cc[:, :, r, :], picked[:, :, :],
                                            wrec[:, :].unsqueeze(2).broadcast_to([P, KB, E]), ALU.mult)
                    i.then_inc(cc_ready, 1)
                if slot == 22:
                    dve.wait_ge(th_ready, pc + 1)
                    v.tensor_scalar(dt_all[:, sl(pc)], zt[:, :], 2.0 * DT_HALF, DT_MID, ALU.mult,
                                    ALU.add).then_inc(dt_ready, 1)
                if slot == 32:
                    dve.wait_ge(chi_ready, pc + 1)
                    v.tensor_tensor(comb[E:P, par(pc)], M[E:P, :], comb[E:P, par(pc)].bitcast(F32),
                                    ALU.subtract).then_inc(clo_ready, 1)

            def mul(c, slot):
                s = c * SLOTS + slot
                m = c * PAIRS + slot
                dve.wait_ge(sq_done, s + 1)
                dve.wait_ge(cb_done, m + 1)
                wait(dve, down_done, s - 1)
                v.tensor_tensor(act[:, slot % 2, :], sq[:, slot % 2, :], CB[:, :], ALU.mult).then_inc(mul_done, 1)

            def ymul(c, n):
                dve.wait_ge(scan_done, c * N + n + 1)
                dve.wait_ge(bcc_done, c * N + n + 1)
                if n == 0:
                    wait(dve, ot_ready, c)
                    dst = yacc[:, :]
                else:
                    wait(dve, yacc_done, c * (N - 1) + n - 2)
                    dst = prod[:, n % 2, :]
                v.tensor_tensor(dst, h[:, n % 2, :], BCC[:, :], ALU.mult).then_inc(ym_done, 1)

            diag = ot[:, :].rearrange("p (k t) -> p k t", k=KB)

            def finish(c):
                dve.wait_ge(down_done, (c + 1) * SLOTS)
                v.tensor_tensor(rest[:, sl(c)], rest[:, sl(c)], DN[:, :], ALU.add).then_inc(rest_done, 1)
                dve.wait_ge(gram_done, (c + 1) * N)
                v.tensor_tensor(diag, GR[:, :].rearrange("p (k t) -> p k t", k=KB),
                                ident[:, :].unsqueeze(1).broadcast_to([P, KB, P]), ALU.mult).then_inc(diag_done, 1)
                dve.wait_ge(diag_done, c + 1)
                v.tensor_reduce(gmax[:, bass.ds(c, 1)], diag, axis=AX.XY, op=ALU.max).then_inc(gmax_done, 1)
                dve.wait_ge(rest_done, c + 1)
                dve.wait_ge(yacc_done, (c + 1) * (N - 1))
                dve.wait_ge(gmax_done, c + 1)
                v.tensor_tensor(ot[:, :], rest[:, sl(c)], yacc[:, :], ALU.add).then_inc(ot_ready, 1)

            def result(c):
                dve.wait_ge(ot_done, c + 1)
                dve.wait_ge(xr_loaded, 16 * (c + 1))
                v.tensor_tensor(res[:, :, :], M[:, :].rearrange("p (k d) -> p k d", k=KB), xr[:, :, :],
                                ALU.add).then_inc(res_ready, 1)

            chains = {}

            def chunk(c, first, last):
                if not last:
                    chains["v"] = Chain(dve, dve_prep, (c + 1) * DVE_PREP)
                for slot in range(SLOTS):
                    n = slot // 2
                    if slot == 0:
                        dve.wait_ge(dtx_ready, c + 1)
                    if slot:
                        if slot <= PAIRS:
                            mul(c, slot - 1)
                    if slot % 2 == 0 and 1 <= n <= N:
                        ymul(c, n - 1)
                    if slot == 1 and not first:
                        finish(c - 1)
                    if slot == 4 and not first:
                        result(c - 1)
                    if slot % 2 == 0 and n < N:
                        dve.wait_ge(bb_done, c * N + n + 1)
                        wait(dve, scan_done, c * N + n)
                        v.tensor_tensor(db[:, :], dtx_all[:, sl(c)], BB[:, :], ALU.mult).then_inc(db_done, 1)
                    if slot % 2 == 1 and n < N:
                        dve.wait_ge(db_done, c * N + n + 1)
                        dve.wait_ge(exp_done, c * N + n + 1)
                        wait(dve, gram_done, c * N + n - 1)
                        wait(dve, carry_done, c * N + max(n - 1, 0))
                        initial = 0.0 if first else carry[:, n:n + 1]
                        v.tensor_tensor_scan(h[:, n % 2, :], decay[:, n % 2, :], db[:, :], initial,
                                             ALU.mult, ALU.add).then_inc(scan_done, 1)
                    if not last:
                        prep(c + 1, slot)
                assert last or chains["v"].n == DVE_PREP, chains["v"].n

            chains["v"] = Chain(dve, dve_prep, 0)
            for slot in range(SLOTS):
                prep(0, slot)
                if slot == 21:
                    dve.wait_ge(up_split, 1)
                    v.tensor_tensor(up_lo[:, :], up_raw[:, :], up_hi[:, :].bitcast(F32), ALU.subtract).then_inc(up_split, 1)
            chunk(0, True, False)
            with dve.Fori(1, NCH - 1) as c:
                chunk(c, False, False)
            chunk(NCH - 1, False, True)
            finish(NCH - 1)
            result(NCH - 1)
            dve.wait_ge(gmax_done, NCH)
            v.tensor_reduce(gm1[:, :], gmax[:, :], axis=AX.X, op=ALU.max).then_inc(g_end, 1)
            dve.wait_ge(g_end, 2)
            v.tensor_reduce(gmt[:, :], GR[0:1, 0:P], axis=AX.X, op=ALU.max).then_inc(g_end, 1)
            dve.wait_ge(g_end, 3)
            v.tensor_scalar(flag[:, :], gmt[:, :], SAFE_SQUARE, None, ALU.is_lt).then_inc(flag_ready, 1)
            dve.wait_ge(flag_ready, 1)
            safe = dve.value_load(flag[0:1, 0:1])
            with dve.If(safe == 0):
                v.memset(ones[:, :], 1.0)
                v.memset(hs[:, :, :], 0.0).then_inc(s_step_dve, 1)
                STEP = 11
                with dve.Fori(0, SEQ) as t:
                    cnt = [0]

                    def link(ins):
                        ins.then_inc(s_step_dve, 1)
                        cnt[0] += 1

                    def linked():
                        dve.wait_ge(s_step_dve, t * STEP + cnt[0] + 1)

                    linked()
                    for b in range(2):
                        i = v.tensor_copy(colb[:, b, :], bc_all[:, bass.ds(t + b * SEQ, 1)].bitcast(F32).broadcast_to([P, P]))
                    i.then_inc(s_col, 1)
                    dve.wait_ge(s_exp, 2 * t + 2)
                    link(v.tensor_tensor(hs[:, :, :], hs[:, :, :], da[:, :, :], ALU.mult))
                    dve.wait_ge(s_bc, t + 1)
                    link(v.tensor_copy(bcs[:, :, :], M[:, 0:4 * N].rearrange("p (b n) -> p b n", b=2)))
                    linked()
                    for b in range(2):
                        link(v.scalar_tensor_tensor(out=hs[:, b, :], in0=bcs[:, b, 0:N], scalar=dtx_all[:, bass.ds(t + b * SEQ, 1)],
                                                    in1=hs[:, b, :], op0=ALU.mult, op1=ALU.add))
                    linked()
                    for b in range(2):
                        i = v.scalar_tensor_tensor(out=junk[:, b, :], in0=hs[:, b, :], scalar=1.0, in1=hs[:, b, :],
                                                   op0=ALU.mult, op1=ALU.mult, accum_out=ss[:, b:b + 1])
                    i.then_inc(s_ss, 1)
                    dve.wait_ge(s_sqrt, t + 1)
                    link(v.tensor_scalar(nrm[:, :], nrm[:, :], 1e-8, None, ALU.add))
                    linked()
                    link(v.reciprocal(scl[:, :], nrm[:, :]))
                    linked()
                    link(v.tensor_scalar(scl[:, :], scl[:, :], NORM_LIMIT, 1.0, ALU.mult, ALU.min))
                    linked()
                    for b in range(2):
                        link(v.tensor_scalar(hs[:, b, :], hs[:, b, :], scl[:, b:b + 1], None, ALU.mult))
                    linked()
                    for b in range(2):
                        link(v.scalar_tensor_tensor(out=junk[:, b, :], in0=hs[:, b, :], scalar=1.0, in1=bcs[:, b, N:2 * N],
                                                    op0=ALU.mult, op1=ALU.mult, accum_out=ss[:, b:b + 1]))
                    linked()
                    for b in range(2):
                        i = v.tensor_copy(dt_all[:, bass.ds(t + b * SEQ, 1)], ss[:, b:b + 1])
                    assert cnt[0] == STEP, cnt[0]
                with dve.Fori(0, NCH) as c:
                    v.tensor_tensor(ot[:, :], rest[:, sl(c)], dt_all[:, sl(c)], ALU.add).then_inc(s_ot, 1)
                    dve.wait_ge(s_otd, c + 1)
                    dve.wait_ge(s_xr, 16 * (c + 1))
                    v.tensor_tensor(res[:, :, :], M[:, :].rearrange("p (k d) -> p k d", k=KB), xr[:, :, :],
                                    ALU.add).then_inc(s_res, 1)

        @block.tensor
        def _(pe):
            mm = nc.tensor.matmul

            def three(dst, hi, lo, cols, start=True, stop=True):
                mm(dst, hi, x_hi[:, cols], start=start, stop=False)
                mm(dst, hi, x_lo[:, cols], start=False, stop=False)
                return mm(dst, lo, x_hi[:, cols], start=False, stop=stop)

            def transposes(src):
                for k in range(KB):
                    i = nc.tensor.transpose(M[:, k * P:(k + 1) * P], src(k), ident[:, :])
                return i

            pe.wait_ge(const_ready, 1)
            pe.wait_ge(w_small, 16 * (2 * (P // (2 * N)) + 1 + P // E))
            for k in range(3):
                nc.tensor.transpose(M[:, k * P:(k + 1) * P], small[:, k, :], ident[:, :]).then_inc(wt_ready, 1)

            def prep(pc, slot):
                if slot == 5:
                    pe.wait_ge(xn_ready, pc + 1)
                    wait(pe, clo_ready, pc)
                    if not isinstance(pc, int) or pc > 1:
                        pe.wait_ge(res_ready, pc - 1)
                    transposes(lambda k: xn[:, k, :]).then_inc(xt_done, 1)
                if slot == 8:
                    pe.wait_ge(xlo_ready, pc + 1)
                    three(M[:, :], proj_hi[:, 0, :], proj_lo[:, 0, :], par(pc)).then_inc(z_done, 1)
                if slot == 10:
                    pe.wait_ge(z_copied, pc + 1)
                    three(M[:, :], proj_hi[:, 1, :], proj_lo[:, 1, :], par(pc)).then_inc(bc_done, 1)
                if slot == 13:
                    pe.wait_ge(bclo_ready, pc + 1)
                    three(M[:, :], proj_hi[:, 2, :], proj_lo[:, 2, :], par(pc)).then_inc(lg_done, 1)
                if slot == 15:
                    pe.wait_ge(lg_copied, pc + 1)
                    alone(pe)
                    for k in range(KB):
                        i = nc.tensor.transpose(M[:, k * E:(k + 1) * E], logit[0:E, k * P:(k + 1) * P], ident[0:E, 0:E])
                    i.then_inc(lgt_done, 1)
                if slot == 30:
                    pe.wait_ge(cc_ready, pc + 1)
                    transposes(lambda k: cc[:, k, :, :].rearrange("p r e -> p (r e)")).then_inc(ct_done, 1)

            def down_mm(c, slot):
                s = c * SLOTS + slot
                if slot < PAIRS:
                    pe.wait_ge(mul_done, c * PAIRS + slot + 1)
                    w = down[:, slot, :]
                else:
                    pe.wait_ge(sq_done, s + 1)
                    w = sdown[:, slot - PAIRS, :]
                mm(DN[:, :], w, act[:, slot % 2, :], start=slot == 0, stop=slot == SLOTS - 1).then_inc(down_done, 1)

            def gram(c, n):
                pe.wait_ge(scan_done, c * N + n + 1)
                if n == 0:
                    wait(pe, diag_done, c)
                pe.wait_ge(ym_done, c * N + n + 1)
                top = h[:, n % 2, :].bitcast(BF16).rearrange("p (t two) -> p t two", two=2)
                for k in range(KB):
                    hb = top[:, k * P:(k + 1) * P, 1]
                    i = mm(GR[:, k * P:(k + 1) * P], hb, hb, start=n == 0 and k == 0,
                           stop=n == N - 1 and k == KB - 1, skip_group_check=True)
                i.then_inc(gram_done, 1)

            def chunk(c, first, last):
                for slot in range(SLOTS):
                    s = c * SLOTS + slot
                    n = slot // 2
                    if slot == 0:
                        pe.wait_ge(xlo_ready, c + 1)
                        pe.wait_ge(clo_ready, c + 1)
                    wait(pe, relu_done, s - 1)
                    w = slice(slot * P, (slot + 1) * P)
                    if slot < PAIRS:
                        three(U[slot % 2][:, :], up_hi[:, w], up_lo[:, w], par(c)).then_inc(up_done, 1)
                    else:
                        w = slice((slot - PAIRS) * P, (slot - PAIRS + 1) * P)
                        three(U[slot % 2][:, :], sup_hi[:, w], sup_lo[:, w], par(c)).then_inc(up_done, 1)
                    if slot >= 2:
                        if slot == 2:
                            wait(pe, rest_done, c)
                        down_mm(c, slot - 2)
                    elif not first:
                        down_mm(c - 1, SLOTS - 2 + slot)
                    if slot % 2 == 0 and n < N:
                        wait(pe, db_done, c * N + n)
                        mm(BB[:, :], onehot_bc[:, n:n + 1].broadcast_to([P, P]), bc_all[:, sl(c)],
                           start=True, stop=True).then_inc(bb_done, 1)
                    if slot % 2 == 1 and n < N:
                        wait(pe, ym_done, c * N + n)
                        mm(BCC[:, :], onehot_bc[:, N + n:N + n + 1].broadcast_to([P, P]), bc_all[:, sl(c)],
                           start=True, stop=True).then_inc(bcc_done, 1)
                    if slot % 2 == 1 and 1 <= n <= N:
                        gram(c, n - 1)
                    if slot < PAIRS:
                        wait(pe, mul_done, c * PAIRS + slot)
                        mm(CB[:, :], onehot_e[:, 2 * slot:2 * slot + 2, :].rearrange("p e i -> p (e i)"),
                           comb[:, par(c)], start=True, stop=True).then_inc(cb_done, 1)
                    if slot == 3 and not first:
                        out_mm(c - 1)
                    if not last:
                        prep(c + 1, slot)

            def out_mm(c):
                pe.wait_ge(ot_ready, c + 1)
                wait(pe, clo_ready, c + 2 if not (isinstance(c, int) and c >= NCH - 2) else NCH)
                transposes(lambda k: ot[:, k * P:(k + 1) * P]).then_inc(ot_done, 1)

            pe.wait_ge(proj_ready, 2)
            for slot in range(SLOTS):
                prep(0, slot)
            pe.wait_ge(up_split, 2)
            pe.wait_ge(w_down, 32)
            pe.wait_ge(dve_init, 3)
            chunk(0, True, False)
            with pe.Fori(1, NCH - 1) as c:
                chunk(c, False, False)
            chunk(NCH - 1, False, True)
            down_mm(NCH - 1, SLOTS - 2)
            down_mm(NCH - 1, SLOTS - 1)
            out_mm(NCH - 1)
            pe.wait_ge(g_end, 1)
            mm(GR[0:1, 0:P], gm1[:, 0:1], ident[:, :], start=True, stop=True).then_inc(g_end, 1)

            pe.wait_ge(flag_ready, 1)
            pe.wait_ge(res_ready, NCH)
            safe = pe.value_load(flag[0:1, 0:1])
            with pe.If(safe == 0):
                with pe.Fori(0, SEQ) as t:
                    pe.wait_ge(s_col, t + 1)
                    for b in range(2):
                        i = mm(M[:, 2 * N * b:2 * N * (b + 1)], colb[:, b, :], onehot_bc[:, :], start=True, stop=True)
                    i.then_inc(s_bc, 1)
                    pe.wait_ge(s_ss, t + 1)
                    mm(M[:, 64:66], ones[:, :], ss[:, :], start=True, stop=True).then_inc(s_norm, 1)
                with pe.Fori(0, NCH) as c:
                    pe.wait_ge(s_ot, c + 1)
                    transposes(lambda k: ot[:, k * P:(k + 1) * P]).then_inc(s_otd, 1)


_INS = ['L0_attn_x', 'L0_attn_Wdt', 'L0_attn_bdt', 'L0_attn_WB', 'L0_attn_WC', 'L0_attn_A_log', 'L0_attn_Dp',
        'L0_ffn_router_w', 'L0_ffn_correction_bias', 'L0_ffn_up_w', 'L0_ffn_down_w', 'L0_ffn_shared_up_w',
        'L0_ffn_shared_down_w']


def kernel(**inputs):
    import concourse.bacc as _bacc
    from concourse.bass_utils import run_bass_kernel_spmd as _run

    nc = _bacc.Bacc("TRN2", target_bir_lowering=False, num_devices=1)
    arrays, args = {}, []
    for name in _INS:
        a = np.ascontiguousarray(inputs[name])
        arrays[f"in_{name}"] = a
        args.append(nc.dram_tensor(f"in_{name}", a.shape, mybir.dt.from_np(a.dtype), kind="ExternalInput").ap())
    out = nc.dram_tensor("out_0", arrays["in_L0_attn_x"].shape, F32, kind="ExternalOutput").ap()
    layer_program(nc, *args, out)
    r = _run(nc, [arrays], core_ids=[0])
    return r.results[0]["out_0"]
```

```python
from contextlib import ExitStack

import numpy as np

import concourse.bass as bass
from concourse import mybir

F32 = mybir.dt.float32
F32R = mybir.dt.float32r
BF16 = mybir.dt.bfloat16
I32 = mybir.dt.int32
ALU = mybir.AluOpType
ACT = mybir.ActivationFunctionType
AX = mybir.AxisListType

P = 128
LOG1P = [0.999999970540657, -0.49999501516787703, 0.33319271342517287, -0.24844369892616386,
         0.19111431081225275, -0.13674769707020493, 0.07836166803754308, -0.029588507405152252,
         0.005253457800249444]
NORM_LIMIT = 20.0
SAFE_SQUARE = NORM_LIMIT * NORM_LIMIT * 0.99
DT_MID, DT_HALF = (0.1 + 0.001) / 2, (0.1 - 0.001) / 2


def layer_program(nc, x_in, wdt_in, bdt_in, wb_in, wc_in, alog_in, dp_in, rw_in, cbias_in,
                  up_in, down_in, sup_in, sdown_in, out):
    BATCH, SEQ, D = x_in.shape
    N = wb_in.shape[0]
    E, _, I = up_in.shape
    SH = sup_in.shape[1]
    T = BATCH * SEQ
    CT = 512
    NCH = T // CT
    CPB = SEQ // CT
    KB = CT // P
    PAIRS = E // 2
    SHP = SH // P
    SLOTS = PAIRS + SHP
    QUARTERS = 4
    G, TOPG = 8, 4
    EG = E // G

    x_flat = x_in.rearrange("b l d -> (b l) d")
    out_flat = out.rearrange("b l d -> (b l) d")

    def x_chunk(c):
        return x_flat[bass.ds(c * CT, CT), :].rearrange("(k p) d -> p k d", p=P)

    def out_chunk(c):
        return out_flat[bass.ds(c * CT, CT), :].rearrange("(k p) d -> p k d", p=P)

    def col(v):
        return v.rearrange("(p a) -> p a", a=1)

    with ExitStack() as ctx:
        def sb(name, shape, dt=F32):
            return ctx.enter_context(nc.sbuf_tensor(name, shape, dt))

        def sem(name):
            return ctx.enter_context(nc.semaphore(name))

        up_hi, up_lo = sb("up_hi", [P, E * I], F32R), sb("up_lo", [P, E * I], F32R)
        down = sb("down", [P, PAIRS, D])
        sup_hi, sup_lo = sb("sup_hi", [P, SH], F32R), sb("sup_lo", [P, SH], F32R)
        sdown = sb("sdown", [P, SHP, D])
        proj_hi, proj_lo = sb("proj_hi", [P, 3, P], F32R), sb("proj_lo", [P, 3, P], F32R)
        onehot_e = sb("onehot_e", [P, E, I], F32R)
        onehot_bc = sb("onehot_bc", [P, 2 * N], F32R)
        ident = sb("ident", [P, P])
        a16 = sb("a16", [P, N])
        dtbias, dtmid = sb("dtbias", [P, 1]), sb("dtmid", [P, 1])
        bdt, dp = sb("bdt", [P, 1]), sb("dp", [P, 1])
        keep = sb("keep", [P, NCH])
        cbias = sb("cbias", [P, E])
        before = sb("before", [P, G, G])
        halves = sb("halves", [P, KB])
        dt_all, dtx_all, rest = sb("dt_all", [P, T]), sb("dtx_all", [P, T]), sb("rest", [P, T])
        bc_all = sb("bc_all", [P, T], F32R)

        x_hi, x_lo = sb("x_hi", [P, 2 * CT], F32R), sb("x_lo", [P, 2 * CT], F32R)
        comb = sb("comb", [P, 2 * CT], F32R)

        xs, xn = sb("xs", [P, KB, D]), sb("xn", [P, KB, D])
        stats, mv = sb("stats", [P, KB, 6]), sb("mv", [P, KB, 2])
        vare, rstd = sb("vare", [P, KB]), sb("rstd", [P, KB])
        xt = sb("xt", [P, CT])
        zt, wexp, poly, zpos = sb("zt", [P, CT]), sb("wexp", [P, CT]), sb("poly", [P, CT]), sb("zpos", [P, CT])
        logit = xn[:, :, :].rearrange("p k d -> p (k d)")
        sig, sfc = sb("sig", [P, KB, E]), sb("sfc", [P, KB, E])
        t4 = sb("t4", [P, 2, KB * G, 4])
        t4a, t4b = t4[:, 0], t4[:, 1]
        t2a, t2b, t2c = sb("t2a", [P, KB * G, 2]), sb("t2b", [P, KB * G, 2]), sb("t2c", [P, KB * G, 2])
        g1a, g1b, g1c = sb("g1a", [P, KB * G]), sb("g1b", [P, KB * G]), sb("g1c", [P, KB * G])
        top8 = sb("top8", [P, KB, 8])
        masked, picked = sb("masked", [P, KB, E]), sb("picked", [P, KB, E])
        cmp_a = t4[:, :, :, :].rearrange("p a g e -> p (a g e)").rearrange("p (g h) -> p g h", h=G)
        cmp_b = picked[:, :, :].rearrange("p k e -> p (k e)").rearrange("p (g h) -> p g h", h=G)
        wsum, wrec = sb("wsum", [P, KB]), sb("wrec", [P, KB])
        cc = sb("cc", [P, KB, 2, E])

        relu, sq, act = sb("relu", [P, 2, CT]), sb("sq", [P, 2, CT]), sb("act", [P, 3, CT])
        decay, db = sb("decay", [P, 2, CT]), sb("db", [P, CT])
        h = sb("h", [P, 2, CT])
        carry = sb("carry", [P, N])
        prod, yacc = sb("prod", [P, 2, CT]), sb("yacc", [P, CT])
        ot, xr, res = sb("ot", [P, CT]), sb("xr", [P, KB, D]), sb("res", [P, KB, D])
        gmax = sb("gmax", [P, NCH])
        gm1, gmt, flag = sb("gm1", [P, 1]), sb("gmt", [1, 1]), sb("flag", [1, 1], I32)
        colb = sb("colb", [P, 2, P], F32R)
        ones = relu[:, 0, 0:P]
        bcs, hs, da = (relu[:, 1, o:o + 2 * w].rearrange("p (b n) -> p b n", b=2)
                       for o, w in ((0, 2 * N), (128, N), (192, N)))
        junk, ss, nrm, scl = sb("junk", [P, 2, N]), sb("ss", [P, 2]), sb("nrm", [P, 2]), sb("scl", [P, 2])

        up_raw = rest
        small = dt_all[:, 0:3 * P].rearrange("p (a k) -> p a k", a=3)
        sup_raw = dt_all[:, 3 * P:3 * P + SH]
        alog = dt_all[:, 1024:1024 + N]
        th = dt_all[:, 1088:1088 + N]
        ea = dt_all[:, 1152:1152 + N]
        ident_r = dtx_all[:, 0:P]
        oh64 = dtx_all[:, P:P + E]
        smallt = dtx_all[:, 512:512 + 3 * P]

        def bank(name):
            return ctx.enter_context(nc.psum_tensor(name, [P, CT], F32))

        U = [bank("U0"), bank("U1")]
        CB = bank("CB")
        DN = bank("DN")
        BB, BCC = bank("BB"), bank("BCC")
        GR = bank("GR")
        M = bank("M")

        w_small, w_late, w_sdown = sem("w_small"), sem("w_late"), sem("w_sdown")
        w_up = [sem(f"w_up{q}") for q in range(QUARTERS)]
        w_down = [sem(f"w_down{q}") for q in range(QUARTERS)]
        const_ready, pool_init = sem("const_ready"), sem("pool_init")
        wt_ready, proj_ready, up_high, up_split, act_init, dve_init = (
            sem("wt_ready"), sem("proj_ready"), sem("up_high"), sem("up_split"), sem("act_init"), sem("dve_init"))
        x_loaded, xr_loaded, stored = sem("x_loaded"), sem("xr_loaded"), sem("stored")
        dve_prep, pool_prep, act_prep = sem("dve_prep"), sem("pool_prep"), sem("act_prep")
        var_ready, rstd_ready, xn_ready = sem("var_ready"), sem("rstd_ready"), sem("xn_ready")
        xt_done, xhi_ready, xlo_ready = sem("xt_done"), sem("xhi_ready"), sem("xlo_ready")
        z_done, z_copied, wexp_ready, sp_ready, th_ready, dt_ready, dtx_ready = (
            sem("z_done"), sem("z_copied"), sem("wexp_ready"), sem("sp_ready"), sem("th_ready"),
            sem("dt_ready"), sem("dtx_ready"))
        bc_done, bchi_ready, bclo_ready = sem("bc_done"), sem("bchi_ready"), sem("bclo_ready")
        lg_done, lg_copied, lgt_done, sig_exp = sem("lg_done"), sem("lg_copied"), sem("lgt_done"), sem("sig_exp")
        cc_ready, ct_done, chi_ready, clo_ready = sem("cc_ready"), sem("ct_done"), sem("chi_ready"), sem("clo_ready")
        up_done, relu_done, sq_done, cb_done, mul_done, down_done = (
            sem("up_done"), sem("relu_done"), sem("sq_done"), sem("cb_done"), sem("mul_done"), sem("down_done"))
        tanh_done, exp_done, bb_done, bcc_done, db_done, scan_done = (
            sem("tanh_done"), sem("exp_done"), sem("bb_done"), sem("bcc_done"), sem("db_done"), sem("scan_done"))
        ym_done, yacc_done, carry_done, gram_done = (
            sem("ym_done"), sem("yacc_done"), sem("carry_done"), sem("gram_done"))
        dn_copied = sem("dn_copied")
        ot_ready, ot_done, res_ready, diag_done, gmax_done = (
            sem("ot_ready"), sem("ot_done"), sem("res_ready"), sem("diag_done"), sem("gmax_done"))
        g_end, flag_ready = sem("g_end"), sem("flag_ready")
        ot_begun = sem("ot_begun")
        passed = sem("passed")
        s_step_dve = sem("s_step_dve")
        s_col, s_bc, s_exp, s_ss, s_norm, s_sqrt, s_ot, s_otd, s_res, s_store, s_xr = (
            sem("s_col"), sem("s_bc"), sem("s_exp"), sem("s_ss"), sem("s_norm"),
            sem("s_sqrt"), sem("s_ot"), sem("s_otd"), sem("s_res"), sem("s_store"), sem("s_xr"))

        def wait(eng, s, value):
            if not isinstance(value, int) or value > 0:
                eng.wait_ge(s, value)

        def alone(eng):
            eng.sem_inc(passed, 1)

        def act_at(slot):
            return zt[:, :] if slot == SLOTS - 1 else act[:, slot % 3, :]

        def sl(c):
            return bass.ds(c * CT, CT)

        def par(c):
            return bass.ds((c % 2) * CT, CT)

        DVE_PREP = 24 + 2 * KB
        POOL_PREP = 18
        ACT_PREP = 1

        SPLIT_AT = [1, 8, 16]

        class Chain:

            def __init__(self, eng, s, base):
                self.eng, self.s, self.base, self.n = eng, s, base, 0

            def then(self, ins):
                ins.then_inc(self.s, 1)
                self.n += 1

            def wait(self, by_itself=False):
                wait(self.eng, self.s, self.base + self.n)
                if by_itself:
                    alone(self.eng)

        block = ctx.enter_context(nc.Block())

        @block.sync
        def _(sp):
            for r in range(P // (2 * N)):
                sp.dma_start(small[2 * N * r:2 * N * r + N, 1, :], wb_in).then_inc(w_small, 16)
                sp.dma_start(small[2 * N * r + N:2 * N * (r + 1), 1, :], wc_in).then_inc(w_small, 16)
            sp.dma_start(small[:, 0, :], wdt_in).then_inc(w_small, 16)
            for r in range(P // E):
                sp.dma_start(small[E * r:E * (r + 1), 2, :], rw_in).then_inc(w_small, 16)
            sp.dma_start(xs[:, :, :], x_chunk(0)).then_inc(x_loaded, 16)
            sp.dma_start(alog, alog_in).then_inc(w_late, 16)
            sp.dma_start(bdt[:, :], col(bdt_in)).then_inc(w_late, 16)
            sp.dma_start(dp[:, :], col(dp_in)).then_inc(w_late, 16)
            sp.dma_start(cbias[:, :], cbias_in.rearrange("(a e) -> a e", a=1).broadcast_to([P, E])).then_inc(w_late, 16)
            sp.dma_start(sup_raw, sup_in).then_inc(w_late, 16)
            for q in range(QUARTERS):
                e0, e1 = q * E // QUARTERS, (q + 1) * E // QUARTERS
                sp.dma_start(up_raw[:, e0 * I:e1 * I].rearrange("p (e i) -> p e i", i=I),
                             up_in[e0:e1].rearrange("e h i -> h e i")).then_inc(w_up[q], 16)
                sp.dma_start(down[:, e0 // 2:e1 // 2, :],
                             down_in[e0:e1].rearrange("(j e) i h -> (e i) j h", e=2)).then_inc(w_down[q], 16)
            sp.dma_start(sdown[:, :, :], sdown_in.rearrange("(j p) h -> p j h", p=P)).then_inc(w_sdown, 16)

            def transfers(c, first, last):
                if not last:
                    wait(sp, xn_ready, c + 1)
                    alone(sp)
                    sp.dma_start(xs[:, :, :], x_chunk(c + 1)).then_inc(x_loaded, 16)
                if not first:
                    sp.dma_start(xr[:, :, :], x_chunk(c - 1)).then_inc(xr_loaded, 16)
                    wait(sp, res_ready, c)
                    alone(sp)
                    sp.dma_start(out_chunk(c - 1), res[:, :, :]).then_inc(stored, 16)
                    sp.wait_ge(stored, 16 * c)
                    alone(sp)

            transfers(0, True, False)
            with sp.Fori(1, NCH - 1) as c:
                transfers(c, False, False)
            transfers(NCH - 1, False, True)
            transfers(NCH, False, True)
            sp.wait_ge(flag_ready, 1)
            safe = sp.value_load(flag[0:1, 0:1])
            with sp.If(safe == 0):
                with sp.Fori(0, NCH) as c:
                    sp.dma_start(xr[:, :, :], x_chunk(c)).then_inc(s_xr, 16)
                    sp.wait_ge(s_res, c + 1)
                    alone(sp)
                    sp.dma_start(out_chunk(c), res[:, :, :]).then_inc(s_store, 16)
                    sp.wait_ge(s_store, 16 * (c + 1))
                    alone(sp)

        @block.gpsimd
        def _(pool):
            g = nc.gpsimd
            n_init = [0]

            def init(ins):
                ins.then_inc(pool_init, 1)
                n_init[0] += 1
                pool.wait_ge(pool_init, n_init[0])

            init(g.memset(ident[:, :], 0.0))
            init(g.affine_select(out=ident[:, :], in_=ident[:, :], compare_op=ALU.not_equal, fill=1.0,
                                 base=0, pattern=[[-1, P]], channel_multiplier=1))
            init(g.memset(oh64, 0.0))
            for base in (0, -E):
                init(g.affine_select(out=oh64, in_=oh64, compare_op=ALU.not_equal, fill=1.0,
                                     base=base, pattern=[[-1, E]], channel_multiplier=1))
            init(g.memset(before[:, :, :], 1.0))
            init(g.affine_select(out=before[:, :, :], in_=before[:, :, :], compare_op=ALU.is_gt, fill=0.0,
                                 base=0, pattern=[[1, G], [-1, G]], channel_multiplier=0))
            init(g.memset(halves[:, :], -0.5))
            init(g.memset(keep[:, :], 1.0))
            for b in range(BATCH):
                init(g.memset(keep[:, b * CPB:b * CPB + 1], 0.0))
            init(g.memset(carry[:, :], 0.0))
            g.memset(gmt[:, :], 0.0).then_inc(const_ready, 1)

            def prep(pc, slot):
                chain = chains["p"]
                if slot == 1:
                    pool.wait_ge(var_ready, pc + 1)
                    alone(pool)
                    chain.then(g.tensor_scalar(vare[:, :], mv[:, :, 1], 1e-5, None, ALU.add))
                    chain.wait(True)
                    g.tensor_tensor(rstd[:, :], vare[:, :], halves[:, :], ALU.pow).then_inc(rstd_ready, 1)
                if slot == 7:
                    pool.wait_ge(xlo_ready, pc + 1)
                    pool.wait_ge(xhi_ready, pc + 1)
                    alone(pool)
                    chain.then(g.tensor_tensor(xt[:, :], x_hi[:, par(pc)].bitcast(F32),
                                               x_lo[:, par(pc)].bitcast(F32), ALU.add))
                if slot == 11:
                    pool.wait_ge(wexp_ready, pc + 1)
                    alone(pool)
                    chain.then(g.tensor_scalar(poly[:, :], wexp[:, :], LOG1P[-1], LOG1P[-2], ALU.mult, ALU.add))
                k, add = divmod(slot - 12, 2)
                if slot >= 12 and k < len(LOG1P) - 1 and not (add and k == len(LOG1P) - 2):
                    chain.wait(True)
                    if add:
                        chain.then(g.tensor_scalar(poly[:, :], poly[:, :], LOG1P[-3 - k], None, ALU.add))
                    else:
                        chain.then(g.tensor_tensor(poly[:, :], poly[:, :], wexp[:, :], ALU.mult))
                if slot == 12 + 2 * (len(LOG1P) - 2) + 1:
                    chain.wait(True)
                    g.tensor_tensor(poly[:, :], poly[:, :], zpos[:, :], ALU.add).then_inc(sp_ready, 1)
                if slot == 30:
                    pool.wait_ge(dt_ready, pc + 1)
                    alone(pool)
                    if isinstance(pc, int) and pc == 0:
                        pool.wait_ge(up_split, 1)
                    g.tensor_tensor(rest[:, sl(pc)], xt[:, :], dp[:, 0:1].broadcast_to([P, CT]), ALU.mult)
                    g.tensor_tensor(dtx_all[:, sl(pc)], dt_all[:, sl(pc)], xt[:, :], ALU.mult).then_inc(dtx_ready, 1)

            def out_begin(c):
                wait(pool, yacc_done, (c + 1) * (N - 1))
                alone(pool)
                g.tensor_tensor(ot[:, :], rest[:, sl(c)], yacc[:, :], ALU.add).then_inc(ot_begun, 1)

            def out_end(c):
                pool.wait_ge(dn_copied, c + 1)
                pool.wait_ge(ot_begun, c + 1)
                alone(pool)
                g.tensor_tensor(rest[:, sl(c)], rest[:, sl(c)], zt[:, :], ALU.add)
                g.tensor_tensor(ot[:, :], ot[:, :], zt[:, :], ALU.add).then_inc(ot_ready, 1)

            def main(c, slot):
                if slot % 2 == 0 and 2 <= slot <= 2 * N:
                    n = slot // 2 - 1
                    pool.wait_ge(scan_done, c * N + n + 1)
                    alone(pool)
                    nxt = NCH - 1 if isinstance(c, int) and c == NCH - 1 else c + 1
                    g.tensor_tensor(carry[:, n:n + 1], h[:, n % 2, CT - 1:CT], keep[:, bass.ds(nxt, 1)],
                                    ALU.mult).then_inc(carry_done, 1)
                    if n:
                        pool.wait_ge(ym_done, c * N + n + 1)
                        wait(pool, yacc_done, c * (N - 1) + n - 1)
                        g.tensor_tensor(yacc[:, :], yacc[:, :], prod[:, n % 2, :], ALU.add).then_inc(yacc_done, 1)

            chains = {}

            def chunk(c, first, last):
                if not last:
                    chains["p"] = Chain(pool, pool_prep, (c + 1) * POOL_PREP)
                for slot in range(SLOTS):
                    if slot == 0 and not first:
                        out_begin(c - 1)
                    if slot == 3 and not first:
                        out_end(c - 1)
                    main(c, slot)
                    if not last:
                        prep(c + 1, slot)
                assert last or chains["p"].n == POOL_PREP, chains["p"].n

            chains["p"] = Chain(pool, pool_prep, 0)
            pool.wait_ge(w_late, 5 * 16)
            pool.wait_ge(act_init, 3)
            for slot in range(SLOTS):
                prep(0, slot)
            chunk(0, True, False)
            with pool.Fori(1, NCH - 1) as c:
                chunk(c, False, False)
            chunk(NCH - 1, False, True)
            out_begin(NCH - 1)
            out_end(NCH - 1)

        @block.scalar
        def _(act_e):
            a = nc.scalar
            act_e.wait_ge(w_late, 5 * 16)
            a.activation(th, alog, ACT.Tanh, scale=0.1).then_inc(act_init, 1)
            act_e.wait_ge(act_init, 1)
            a.activation(ea, th, ACT.Exp, scale=10.0).then_inc(act_init, 1)
            a.activation(sup_hi[:, :], sup_raw, ACT.Copy).then_inc(act_init, 1)
            act_e.wait_ge(wt_ready, 3)
            a.activation(proj_hi[:, :, :].rearrange("p a k -> p (a k)"), M[:, 0:3 * P], ACT.Copy).then_inc(proj_ready, 1)

            def prep(pc, slot):
                if slot == 6:
                    act_e.wait_ge(xt_done, pc + 1)
                    alone(act_e)
                    a.activation(x_hi[:, par(pc)], M[:, :], ACT.Copy).then_inc(xhi_ready, 1)
                if slot == 9:
                    act_e.wait_ge(z_done, pc + 1)
                    wait(act_e, sp_ready, pc)
                    if not isinstance(pc, int) or pc > 1:
                        act_e.wait_ge(ot_ready, pc - 1)
                    a.activation(zt[:, :], M[:, :], ACT.Identity, bias=bdt[:, 0:1]).then_inc(z_copied, 1)
                    act_e.wait_ge(z_copied, pc + 1)
                    a.activation(zpos[:, :], zt[:, :], ACT.Relu)
                    a.activation(wexp[:, :], zt[:, :], ACT.Abs).then_inc(act_prep, 1)
                if slot == 10:
                    act_e.wait_ge(act_prep, pc + 1)
                    a.activation(wexp[:, :], wexp[:, :], ACT.Exp, scale=-1.0).then_inc(wexp_ready, 1)
                if slot == 16:
                    act_e.wait_ge(bc_done, pc + 1)
                    alone(act_e)
                    a.activation(bc_all[:, sl(pc)], M[:, :], ACT.Copy).then_inc(bchi_ready, 1)
                if slot == 11:
                    act_e.wait_ge(lg_done, pc + 1)
                    a.activation(logit[:, :], M[:, :], ACT.Copy).then_inc(lg_copied, 1)
                if slot == 13:
                    act_e.wait_ge(lgt_done, pc + 1)
                    a.activation(sig[:, :, :].rearrange("p k e -> p (k e)"), M[:, 0:KB * E], ACT.Exp,
                                 scale=-1.0).then_inc(sig_exp, 1)
                if slot == 28:
                    act_e.wait_ge(sp_ready, pc + 1)
                    a.activation(zt[:, :], poly[:, :], ACT.Tanh, scale=0.5 / DT_HALF,
                                 bias=dtbias[:, 0:1]).then_inc(th_ready, 1)
                if slot == 29:
                    act_e.wait_ge(th_ready, pc + 1)
                    alone(act_e)
                    a.activation(dt_all[:, sl(pc)], zt[:, :], ACT.Identity, scale=2.0 * DT_HALF,
                                 bias=dtmid[:, 0:1]).then_inc(dt_ready, 1)
                if slot == 32:
                    act_e.wait_ge(ct_done, pc + 1)
                    alone(act_e)
                    a.activation(comb[:, par(pc)], M[:, :], ACT.Copy).then_inc(chi_ready, 1)

            def main(c, slot):
                s = c * SLOTS + slot
                n = slot // 2
                act_e.wait_ge(up_done, s + 1)
                wait(act_e, sq_done, s - 1)
                a.activation(relu[:, slot % 2, :], U[slot % 2][:, :], ACT.Relu).then_inc(relu_done, 1)
                if n < N and slot % 2 == 0:
                    wait(act_e, scan_done, c * N + n - 1)
                    alone(act_e)
                    a.activation(decay[:, n % 2, :], dt_all[:, sl(c)], ACT.Tanh, scale=a16[:, n:n + 1]).then_inc(tanh_done, 1)
                if n < N and slot % 2 == 1:
                    act_e.wait_ge(tanh_done, c * N + n + 1)
                    a.activation(decay[:, n % 2, :], decay[:, n % 2, :], ACT.Exp, scale=16.0).then_inc(exp_done, 1)
                act_e.wait_ge(relu_done, s + 1)
                if slot < PAIRS:
                    wait(act_e, mul_done, c * PAIRS + slot - 1)
                    dst = sq[:, slot % 2, :]
                else:
                    act_e.wait_ge(down_done, s - 2)
                    if slot == SLOTS - 1:
                        act_e.wait_ge(dt_ready, c + 1)
                    dst = act_at(slot)
                a.activation(dst, relu[:, slot % 2, :], ACT.Square).then_inc(sq_done, 1)

            def dn_copy(c):
                act_e.wait_ge(down_done, (c + 1) * SLOTS)
                a.activation(zt[:, :], DN[:, :], ACT.Copy).then_inc(dn_copied, 1)

            def split_up(q):
                cols = slice(q * E * I // QUARTERS, (q + 1) * E * I // QUARTERS)
                act_e.wait_ge(w_up[q], 16)
                a.activation(up_hi[:, cols], up_raw[:, cols], ACT.Copy).then_inc(up_high, 1)

            def chunk(c, first, last):
                for slot in range(SLOTS):
                    if slot == 3 and not first:
                        dn_copy(c - 1)
                    if first and slot in SPLIT_AT:
                        split_up(1 + SPLIT_AT.index(slot))
                    if slot == 0:
                        act_e.wait_ge(dt_ready, c + 1)
                    main(c, slot)
                    if not last:
                        prep(c + 1, slot)

            act_e.wait_ge(dve_init, 3)
            for slot in range(SLOTS):
                if slot == 19:
                    split_up(0)
                prep(0, slot)
            chunk(0, True, False)
            with act_e.Fori(1, NCH - 1) as c:
                chunk(c, False, False)
            chunk(NCH - 1, False, True)
            dn_copy(NCH - 1)

            act_e.wait_ge(flag_ready, 1)
            safe = act_e.value_load(flag[0:1, 0:1])
            with act_e.If(safe == 0):
                with act_e.Fori(0, SEQ) as t:
                    for b in range(2):
                        i = a.activation(da[:, b, :], a16[:, :], ACT.Tanh, scale=dt_all[:, bass.ds(t + b * SEQ, 1)])
                    i.then_inc(s_exp, 1)
                    act_e.wait_ge(s_exp, 2 * t + 1)
                    a.activation(da[:, :, :], da[:, :, :], ACT.Exp, scale=16.0).then_inc(s_exp, 1)
                    act_e.wait_ge(s_norm, t + 1)
                    a.activation(nrm[:, :], M[:, 64:66], ACT.Sqrt).then_inc(s_sqrt, 1)

        @block.vector
        def _(dve):
            v = nc.vector
            dve.wait_ge(act_init, 3)
            v.tensor_scalar(a16[:, :], ea, -1.0 / 16, None, ALU.mult).then_inc(dve_init, 1)
            v.memset(dtbias[:, :], -0.5 * DT_MID / DT_HALF).then_inc(dve_init, 1)
            v.memset(dtmid[:, :], DT_MID).then_inc(dve_init, 1)
            v.tensor_tensor(sup_lo[:, :], sup_raw, sup_hi[:, :].bitcast(F32), ALU.subtract)
            dve.wait_ge(const_ready, 1)
            v.tensor_copy(onehot_bc[:, :], oh64[:, 0:2 * N])
            v.tensor_copy(onehot_e[:, :, :], oh64.unsqueeze(2).broadcast_to([P, E, I])).then_inc(dve_init, 1)
            dve.wait_ge(proj_ready, 1)
            v.tensor_tensor(proj_lo[:, :, :].rearrange("p a k -> p (a k)"), M[:, 0:3 * P],
                            proj_hi[:, :, :].rearrange("p a k -> p (a k)").bitcast(F32), ALU.subtract).then_inc(proj_ready, 1)

            def dup(t, n):
                return t.unsqueeze(2).broadcast_to([P, KB * G, n])

            sfc_g = sfc[:, :, :].rearrange("p k (g e) -> p (k g) e", g=G)
            gs3 = g1a[:, :].rearrange("p (k g) -> p k g", g=G)
            c3 = cmp_a[:, :, :].rearrange("p (k g) h -> p k g h", g=G)
            d3 = cmp_b[:, :, :].rearrange("p (k g) h -> p k g h", g=G)

            def gs_h():
                return gs3.unsqueeze(2).broadcast_to([P, KB, G, G])

            def gs_g():
                return gs3.unsqueeze(3).broadcast_to([P, KB, G, G])

            def prep(pc, slot):
                ch = chains["v"]

                def op(f, *args, **kw):
                    ch.wait(f in (v.max, v.match_replace))
                    ch.then(f(*args, **kw))

                if slot == 1:
                    dve.wait_ge(x_loaded, 16 * (pc + 1))
                    for k in range(KB):
                        i = v.bn_stats(stats[:, k, :], xs[:, k, :])
                    ch.then(i)
                    ch.wait(True)
                    for k in range(KB):
                        i = v.bn_aggr(mv[:, k, :], stats[:, k, :])
                    i.then_inc(var_ready, 1)
                if slot == 3:
                    dve.wait_ge(rstd_ready, pc + 1)
                    wait(dve, lgt_done, pc)
                    for k in range(KB):
                        i = v.tensor_scalar(xn[:, k, :], xs[:, k, :], mv[:, k, 0:1], rstd[:, k:k + 1],
                                            ALU.subtract, ALU.mult)
                    i.then_inc(xn_ready, 1)
                if slot == 7:
                    dve.wait_ge(xhi_ready, pc + 1)
                    v.tensor_tensor(x_lo[:, par(pc)], M[:, :], x_hi[:, par(pc)].bitcast(F32),
                                    ALU.subtract).then_inc(xlo_ready, 1)
                if slot == 17:
                    dve.wait_ge(bchi_ready, pc + 1)
                    v.tensor_tensor(bc_all[E:P, sl(pc)], M[E:P, :], bc_all[E:P, sl(pc)].bitcast(F32),
                                    ALU.subtract).then_inc(bclo_ready, 1)
                if slot == 14:
                    dve.wait_ge(sig_exp, pc + 1)
                    ch.then(v.tensor_scalar(sig[:, :, :], sig[:, :, :], 1.0, None, ALU.add))
                if slot == 15:
                    op(v.reciprocal, sig[:, 0:KB // 2, :], sig[:, 0:KB // 2, :])
                if slot == 16:
                    op(v.reciprocal, sig[:, KB // 2:KB, :], sig[:, KB // 2:KB, :])
                if slot == 18:
                    op(v.tensor_tensor, sfc[:, :, :], sig[:, :, :],
                       cbias[:, :].unsqueeze(1).broadcast_to([P, KB, E]), ALU.add)
                if slot == 19:
                    ch.wait()
                    v.tensor_tensor(t4a[:, :, :], sfc_g[:, :, 0:4], sfc_g[:, :, 4:8], ALU.max)
                    ch.then(v.tensor_tensor(t4b[:, :, :], sfc_g[:, :, 0:4], sfc_g[:, :, 4:8], ALU.min))
                    ch.wait()
                    v.tensor_tensor(t2a[:, :, :], t4a[:, :, 0:2], t4a[:, :, 2:4], ALU.max)
                    v.tensor_tensor(t2b[:, :, :], t4a[:, :, 0:2], t4a[:, :, 2:4], ALU.min)
                    ch.then(v.tensor_tensor(t2c[:, :, :], t4b[:, :, 0:2], t4b[:, :, 2:4], ALU.max))
                    op(v.tensor_tensor, t2b[:, :, :], t2b[:, :, :], t2c[:, :, :], ALU.max)
                if slot == 20:
                    ch.wait()
                    v.tensor_tensor(g1a[:, :], t2a[:, :, 0], t2a[:, :, 1], ALU.max)
                    v.tensor_tensor(g1b[:, :], t2a[:, :, 0], t2a[:, :, 1], ALU.min)
                    ch.then(v.tensor_tensor(g1c[:, :], t2b[:, :, 0], t2b[:, :, 1], ALU.max))
                    op(v.tensor_tensor, g1b[:, :], g1b[:, :], g1c[:, :], ALU.max)
                    op(v.tensor_tensor, g1a[:, :], g1a[:, :], g1b[:, :], ALU.add)
                if slot == 22:
                    ch.wait()
                    v.tensor_tensor(c3, gs_h(), gs_g(), ALU.is_gt)
                    ch.then(v.tensor_tensor(d3, gs_h(), gs_g(), ALU.is_equal))
                if slot == 23:
                    op(v.tensor_tensor, d3, d3, before[:, :, :].unsqueeze(1).broadcast_to([P, KB, G, G]), ALU.mult)
                    op(v.tensor_tensor, cmp_a[:, :, :], cmp_a[:, :, :], cmp_b[:, :, :], ALU.add)
                if slot == 24:
                    op(v.tensor_reduce, g1b[:, :], cmp_a[:, :, :], axis=AX.X, op=ALU.add)
                    op(v.tensor_scalar, g1c[:, :], g1b[:, :], TOPG - 0.5, None, ALU.is_lt)
                if slot == 25:
                    op(v.tensor_tensor, masked[:, :, :].rearrange("p k (g e) -> p (k g) e", g=G), sfc_g,
                       dup(g1c[:, :], EG), ALU.mult)
                    op(v.tensor_scalar, masked[:, :, :], masked[:, :, :], 0.0, None, ALU.add)
                if 26 <= slot < 26 + KB:
                    k = slot - 26
                    op(v.max, top8[:, k, :], masked[:, k, :])
                    op(v.match_replace, out=picked[:, k, :], in_to_replace=top8[:, k, :], in_values=masked[:, k, :],
                       imm_value=-3.0e38)
                if slot == 30:
                    op(v.tensor_tensor, picked[:, :, :], picked[:, :, :], masked[:, :, :], ALU.not_equal)
                    op(v.tensor_tensor, picked[:, :, :], picked[:, :, :], sig[:, :, :], ALU.mult)
                    op(v.tensor_reduce, wsum[:, :], picked[:, :, :], axis=AX.X, op=ALU.add)
                if slot == 31:
                    op(v.tensor_scalar, wsum[:, :], wsum[:, :], 1e-20, None, ALU.add)
                    op(v.reciprocal, wrec[:, :], wsum[:, :])
                    op(v.tensor_scalar, wrec[:, :], wrec[:, :], 2.5, None, ALU.mult)
                if slot == 31:
                    ch.wait()
                    wait(dve, ct_done, pc)
                    for r in range(2):
                        i = v.tensor_tensor(cc[:, :, r, :], picked[:, :, :],
                                            wrec[:, :].unsqueeze(2).broadcast_to([P, KB, E]), ALU.mult)
                    i.then_inc(cc_ready, 1)
                if slot == 33:
                    dve.wait_ge(chi_ready, pc + 1)
                    v.tensor_tensor(comb[E:P, par(pc)], M[E:P, :], comb[E:P, par(pc)].bitcast(F32),
                                    ALU.subtract).then_inc(clo_ready, 1)

            def mul(c, slot):
                s = c * SLOTS + slot
                m = c * PAIRS + slot
                dve.wait_ge(sq_done, s + 1)
                dve.wait_ge(cb_done, m + 1)
                wait(dve, down_done, s - 2)
                v.tensor_tensor(act_at(slot), sq[:, slot % 2, :], CB[:, :], ALU.mult).then_inc(mul_done, 1)

            def ymul(c, n):
                dve.wait_ge(scan_done, c * N + n + 1)
                dve.wait_ge(bcc_done, c * N + n + 1)
                if n == 0:
                    wait(dve, ot_begun, c)
                    dst = yacc[:, :]
                else:
                    wait(dve, yacc_done, c * (N - 1) + n - 2)
                    dst = prod[:, n % 2, :]
                v.tensor_tensor(dst, h[:, n % 2, :], BCC[:, :], ALU.mult).then_inc(ym_done, 1)

            diag = res[:, :, :]

            def norms(c, part):
                if part == 0:
                    dve.wait_ge(gram_done, (c + 1) * N)
                    if not isinstance(c, int) or c > 0:
                        dve.wait_ge(xr_loaded, 16 * (c + 1))
                    v.tensor_tensor(diag, GR[:, :].rearrange("p (k t) -> p k t", k=KB),
                                    ident[:, :].unsqueeze(1).broadcast_to([P, KB, P]), ALU.mult).then_inc(diag_done, 1)
                else:
                    dve.wait_ge(diag_done, c + 1)
                    v.tensor_reduce(gmax[:, bass.ds(c, 1)], diag, axis=AX.XY, op=ALU.max).then_inc(gmax_done, 1)

            def result(c):
                dve.wait_ge(ot_done, c + 1)
                dve.wait_ge(xr_loaded, 16 * (c + 1))
                dve.wait_ge(gmax_done, c + 1)
                v.tensor_tensor(res[:, :, :], M[:, :].rearrange("p (k d) -> p k d", k=KB), xr[:, :, :],
                                ALU.add).then_inc(res_ready, 1)

            def split_up(q):
                cols = slice(q * E * I // QUARTERS, (q + 1) * E * I // QUARTERS)
                dve.wait_ge(up_high, q + 1)
                v.tensor_tensor(up_lo[:, cols], up_raw[:, cols], up_hi[:, cols].bitcast(F32),
                                ALU.subtract).then_inc(up_split, 1)

            chains = {}

            def chunk(c, first, last):
                if not last:
                    chains["v"] = Chain(dve, dve_prep, (c + 1) * DVE_PREP)
                for slot in range(SLOTS):
                    n = slot // 2
                    if slot == 0:
                        dve.wait_ge(dtx_ready, c + 1)
                    if slot:
                        if slot <= PAIRS:
                            mul(c, slot - 1)
                    if slot % 2 == 0 and 1 <= n <= N:
                        ymul(c, n - 1)
                    if slot < 2 and not first:
                        norms(c - 1, slot)
                    if slot == 21 and not first:
                        result(c - 1)
                    if first and slot in SPLIT_AT:
                        split_up(1 + SPLIT_AT.index(slot))
                    if slot % 2 == 0 and n < N:
                        dve.wait_ge(bb_done, c * N + n + 1)
                        wait(dve, scan_done, c * N + n)
                        v.tensor_tensor(db[:, :], dtx_all[:, sl(c)], BB[:, :], ALU.mult).then_inc(db_done, 1)
                    if slot % 2 == 1 and n < N:
                        dve.wait_ge(db_done, c * N + n + 1)
                        dve.wait_ge(exp_done, c * N + n + 1)
                        wait(dve, gram_done, c * N + n - 1)
                        wait(dve, carry_done, c * N + max(n - 1, 0))
                        initial = 0.0 if first else carry[:, n:n + 1]
                        v.tensor_tensor_scan(h[:, n % 2, :], decay[:, n % 2, :], db[:, :], initial,
                                             ALU.mult, ALU.add).then_inc(scan_done, 1)
                    if not last:
                        prep(c + 1, slot)
                assert last or chains["v"].n == DVE_PREP, chains["v"].n

            chains["v"] = Chain(dve, dve_prep, 0)
            for slot in range(SLOTS):
                prep(0, slot)
                if slot == 30:
                    split_up(0)
            chunk(0, True, False)
            with dve.Fori(1, NCH - 1) as c:
                chunk(c, False, False)
            chunk(NCH - 1, False, True)
            norms(NCH - 1, 0)
            norms(NCH - 1, 1)
            result(NCH - 1)
            dve.wait_ge(gmax_done, NCH)
            v.tensor_reduce(gm1[:, :], gmax[:, :], axis=AX.X, op=ALU.max).then_inc(g_end, 1)
            dve.wait_ge(g_end, 2)
            v.tensor_reduce(gmt[:, :], GR[0:1, 0:P], axis=AX.X, op=ALU.max).then_inc(g_end, 1)
            dve.wait_ge(g_end, 3)
            v.tensor_scalar(flag[:, :], gmt[:, :], SAFE_SQUARE, None, ALU.is_lt).then_inc(flag_ready, 1)
            dve.wait_ge(flag_ready, 1)
            safe = dve.value_load(flag[0:1, 0:1])
            with dve.If(safe == 0):
                v.memset(ones[:, :], 1.0)
                v.memset(hs[:, :, :], 0.0).then_inc(s_step_dve, 1)
                STEP = 11
                with dve.Fori(0, SEQ) as t:
                    cnt = [0]

                    def link(ins):
                        ins.then_inc(s_step_dve, 1)
                        cnt[0] += 1

                    def linked():
                        dve.wait_ge(s_step_dve, t * STEP + cnt[0] + 1)

                    linked()
                    for b in range(2):
                        i = v.tensor_copy(colb[:, b, :], bc_all[:, bass.ds(t + b * SEQ, 1)].bitcast(F32).broadcast_to([P, P]))
                    i.then_inc(s_col, 1)
                    dve.wait_ge(s_exp, 2 * t + 2)
                    link(v.tensor_tensor(hs[:, :, :], hs[:, :, :], da[:, :, :], ALU.mult))
                    dve.wait_ge(s_bc, t + 1)
                    link(v.tensor_copy(bcs[:, :, :], M[:, 0:4 * N].rearrange("p (b n) -> p b n", b=2)))
                    linked()
                    for b in range(2):
                        link(v.scalar_tensor_tensor(out=hs[:, b, :], in0=bcs[:, b, 0:N], scalar=dtx_all[:, bass.ds(t + b * SEQ, 1)],
                                                    in1=hs[:, b, :], op0=ALU.mult, op1=ALU.add))
                    linked()
                    for b in range(2):
                        i = v.scalar_tensor_tensor(out=junk[:, b, :], in0=hs[:, b, :], scalar=1.0, in1=hs[:, b, :],
                                                   op0=ALU.mult, op1=ALU.mult, accum_out=ss[:, b:b + 1])
                    i.then_inc(s_ss, 1)
                    dve.wait_ge(s_sqrt, t + 1)
                    link(v.tensor_scalar(nrm[:, :], nrm[:, :], 1e-8, None, ALU.add))
                    linked()
                    link(v.reciprocal(scl[:, :], nrm[:, :]))
                    linked()
                    link(v.tensor_scalar(scl[:, :], scl[:, :], NORM_LIMIT, 1.0, ALU.mult, ALU.min))
                    linked()
                    for b in range(2):
                        link(v.tensor_scalar(hs[:, b, :], hs[:, b, :], scl[:, b:b + 1], None, ALU.mult))
                    linked()
                    for b in range(2):
                        link(v.scalar_tensor_tensor(out=junk[:, b, :], in0=hs[:, b, :], scalar=1.0, in1=bcs[:, b, N:2 * N],
                                                    op0=ALU.mult, op1=ALU.mult, accum_out=ss[:, b:b + 1]))
                    linked()
                    for b in range(2):
                        i = v.tensor_copy(dt_all[:, bass.ds(t + b * SEQ, 1)], ss[:, b:b + 1])
                    assert cnt[0] == STEP, cnt[0]
                with dve.Fori(0, NCH) as c:
                    v.tensor_tensor(ot[:, :], rest[:, sl(c)], dt_all[:, sl(c)], ALU.add).then_inc(s_ot, 1)
                    dve.wait_ge(s_otd, c + 1)
                    dve.wait_ge(s_xr, 16 * (c + 1))
                    v.tensor_tensor(res[:, :, :], M[:, :].rearrange("p (k d) -> p k d", k=KB), xr[:, :, :],
                                    ALU.add).then_inc(s_res, 1)

        @block.tensor
        def _(pe):
            mm = nc.tensor.matmul

            def three(dst, hi, lo, cols, start=True, stop=True):
                mm(dst, hi, x_hi[:, cols], start=start, stop=False)
                mm(dst, hi, x_lo[:, cols], start=False, stop=False)
                return mm(dst, lo, x_hi[:, cols], start=False, stop=stop)

            def transposes(src):
                for k in range(KB):
                    i = nc.tensor.transpose(M[:, k * P:(k + 1) * P], src(k), ident[:, :])
                return i

            pe.wait_ge(const_ready, 1)
            pe.wait_ge(w_small, 16 * (2 * (P // (2 * N)) + 1 + P // E))
            for k in range(3):
                nc.tensor.transpose(M[:, k * P:(k + 1) * P], small[:, k, :], ident[:, :]).then_inc(wt_ready, 1)

            def prep(pc, slot):
                if slot == 5:
                    pe.wait_ge(xn_ready, pc + 1)
                    wait(pe, clo_ready, pc)
                    transposes(lambda k: xn[:, k, :]).then_inc(xt_done, 1)
                if slot == 8:
                    pe.wait_ge(xlo_ready, pc + 1)
                    three(M[:, :], proj_hi[:, 0, :], proj_lo[:, 0, :], par(pc)).then_inc(z_done, 1)
                if slot == 15:
                    pe.wait_ge(sig_exp, pc + 1)
                    three(M[:, :], proj_hi[:, 1, :], proj_lo[:, 1, :], par(pc)).then_inc(bc_done, 1)
                if slot == 10:
                    pe.wait_ge(z_copied, pc + 1)
                    three(M[:, :], proj_hi[:, 2, :], proj_lo[:, 2, :], par(pc)).then_inc(lg_done, 1)
                if slot == 12:
                    pe.wait_ge(lg_copied, pc + 1)
                    alone(pe)
                    for k in range(KB):
                        i = nc.tensor.transpose(M[:, k * E:(k + 1) * E], logit[0:E, k * P:(k + 1) * P], ident[0:E, 0:E])
                    i.then_inc(lgt_done, 1)
                if slot == 32:
                    pe.wait_ge(cc_ready, pc + 1)
                    if not isinstance(pc, int) or pc > 1:
                        pe.wait_ge(res_ready, pc - 1)
                    transposes(lambda k: cc[:, k, :, :].rearrange("p r e -> p (r e)")).then_inc(ct_done, 1)

            def down_mm(c, slot):
                s = c * SLOTS + slot
                if slot < PAIRS:
                    pe.wait_ge(mul_done, c * PAIRS + slot + 1)
                    w, a = down[:, slot, :], act_at(slot)
                else:
                    pe.wait_ge(sq_done, s + 1)
                    w, a = sdown[:, slot - PAIRS, :], act_at(slot)
                mm(DN[:, :], w, a, start=slot == 0, stop=slot == SLOTS - 1).then_inc(down_done, 1)

            def cb_mm(c, slot):
                wait(pe, mul_done, c * PAIRS + slot)
                mm(CB[:, :], onehot_e[:, 2 * slot:2 * slot + 2, :].rearrange("p e i -> p (e i)"),
                   comb[:, par(c)], start=True, stop=True).then_inc(cb_done, 1)

            def gram(c, n):
                pe.wait_ge(scan_done, c * N + n + 1)
                if n == 0:
                    wait(pe, diag_done, c)
                pe.wait_ge(ym_done, c * N + n + 1)
                top = h[:, n % 2, :].bitcast(BF16).rearrange("p (t two) -> p t two", two=2)
                for k in range(KB):
                    hb = top[:, k * P:(k + 1) * P, 1]
                    i = mm(GR[:, k * P:(k + 1) * P], hb, hb, start=n == 0 and k == 0,
                           stop=n == N - 1 and k == KB - 1, skip_group_check=True)
                i.then_inc(gram_done, 1)

            def chunk(c, first, last):
                for slot in range(SLOTS):
                    s = c * SLOTS + slot
                    n = slot // 2
                    if slot == 0:
                        pe.wait_ge(xlo_ready, c + 1)
                    if first and slot % (PAIRS // QUARTERS) == 0 and slot < PAIRS:
                        pe.wait_ge(up_split, slot // (PAIRS // QUARTERS) + 1)
                    wait(pe, relu_done, s - 1)
                    w = slice(slot * P, (slot + 1) * P)
                    if slot < PAIRS:
                        three(U[slot % 2][:, :], up_hi[:, w], up_lo[:, w], par(c)).then_inc(up_done, 1)
                    else:
                        w = slice((slot - PAIRS) * P, (slot - PAIRS + 1) * P)
                        three(U[slot % 2][:, :], sup_hi[:, w], sup_lo[:, w], par(c)).then_inc(up_done, 1)
                    if 1 <= slot <= PAIRS:
                        if slot == 1:
                            pe.wait_ge(clo_ready, c + 1)
                        cb_mm(c, slot - 1)
                    if 3 < slot:
                        if first and (slot - 3) % (PAIRS // QUARTERS) == 0 and slot - 3 < PAIRS:
                            pe.wait_ge(w_down[(slot - 3) // (PAIRS // QUARTERS)], 16)
                        down_mm(c, slot - 3)
                    elif slot < 3 and not first:
                        down_mm(c - 1, SLOTS - 3 + slot)
                    if slot % 2 == 0 and n < N:
                        wait(pe, db_done, c * N + n)
                        mm(BB[:, :], onehot_bc[:, n:n + 1].broadcast_to([P, P]), bc_all[:, sl(c)],
                           start=True, stop=True).then_inc(bb_done, 1)
                    if slot % 2 == 1 and n < N:
                        wait(pe, ym_done, c * N + n)
                        mm(BCC[:, :], onehot_bc[:, N + n:N + n + 1].broadcast_to([P, P]), bc_all[:, sl(c)],
                           start=True, stop=True).then_inc(bcc_done, 1)
                    if slot % 2 == 1 and 1 <= n <= N:
                        gram(c, n - 1)
                    if slot == 3:
                        if first:
                            pe.wait_ge(w_down[0], 16)
                        wait(pe, dn_copied, c)
                        down_mm(c, 0)
                    if slot == 19 and not first:
                        out_mm(c - 1, last)
                    if not last:
                        prep(c + 1, slot)

            def out_mm(c, last):
                pe.wait_ge(ot_ready, c + 1)
                if last:
                    pe.wait_ge(clo_ready, NCH)
                    wait(pe, res_ready, c)
                else:
                    pe.wait_ge(bclo_ready, c + 3)
                transposes(lambda k: ot[:, k * P:(k + 1) * P]).then_inc(ot_done, 1)

            pe.wait_ge(proj_ready, 2)
            for slot in range(SLOTS):
                prep(0, slot)
            pe.wait_ge(dve_init, 4)
            pe.wait_ge(w_sdown, 16)
            chunk(0, True, False)
            with pe.Fori(1, NCH - 1) as c:
                chunk(c, False, False)
            chunk(NCH - 1, False, True)
            for slot in (3, 2, 1):
                down_mm(NCH - 1, SLOTS - slot)
            out_mm(NCH - 1, True)
            pe.wait_ge(g_end, 1)
            mm(GR[0:1, 0:P], gm1[:, 0:1], ident[:, :], start=True, stop=True).then_inc(g_end, 1)

            pe.wait_ge(flag_ready, 1)
            pe.wait_ge(res_ready, NCH)
            safe = pe.value_load(flag[0:1, 0:1])
            with pe.If(safe == 0):
                with pe.Fori(0, SEQ) as t:
                    pe.wait_ge(s_col, t + 1)
                    for b in range(2):
                        i = mm(M[:, 2 * N * b:2 * N * (b + 1)], colb[:, b, :], onehot_bc[:, :], start=True, stop=True)
                    i.then_inc(s_bc, 1)
                    pe.wait_ge(s_ss, t + 1)
                    mm(M[:, 64:66], ones[:, :], ss[:, :], start=True, stop=True).then_inc(s_norm, 1)
                with pe.Fori(0, NCH) as c:
                    pe.wait_ge(s_ot, c + 1)
                    transposes(lambda k: ot[:, k * P:(k + 1) * P]).then_inc(s_otd, 1)


_INS = ['L0_attn_x', 'L0_attn_Wdt', 'L0_attn_bdt', 'L0_attn_WB', 'L0_attn_WC', 'L0_attn_A_log', 'L0_attn_Dp',
        'L0_ffn_router_w', 'L0_ffn_correction_bias', 'L0_ffn_up_w', 'L0_ffn_down_w', 'L0_ffn_shared_up_w',
        'L0_ffn_shared_down_w']


def kernel(**inputs):
    import concourse.bacc as _bacc
    from concourse.bass_utils import run_bass_kernel_spmd as _run

    nc = _bacc.Bacc("TRN2", target_bir_lowering=False, num_devices=1)
    arrays, args = {}, []
    for name in _INS:
        a = np.ascontiguousarray(inputs[name])
        arrays[f"in_{name}"] = a
        args.append(nc.dram_tensor(f"in_{name}", a.shape, mybir.dt.from_np(a.dtype), kind="ExternalInput").ap())
    out = nc.dram_tensor("out_0", arrays["in_L0_attn_x"].shape, F32, kind="ExternalOutput").ap()
    layer_program(nc, *args, out)
    r = _run(nc, [arrays], core_ids=[0])
    return r.results[0]["out_0"]
```

```python
from contextlib import ExitStack

import numpy as np

import concourse.bass as bass
from concourse import mybir

F32 = mybir.dt.float32
F32R = mybir.dt.float32r
BF16 = mybir.dt.bfloat16
I32 = mybir.dt.int32
ALU = mybir.AluOpType
ACT = mybir.ActivationFunctionType
AX = mybir.AxisListType

P = 128
LOG1P = [0.999999970540657, -0.49999501516787703, 0.33319271342517287, -0.24844369892616386,
         0.19111431081225275, -0.13674769707020493, 0.07836166803754308, -0.029588507405152252,
         0.005253457800249444]
NORM_LIMIT = 20.0
SAFE_SQUARE = NORM_LIMIT * NORM_LIMIT * 0.99
DT_MID, DT_HALF = (0.1 + 0.001) / 2, (0.1 - 0.001) / 2


def layer_program(nc, x_in, wdt_in, bdt_in, wb_in, wc_in, alog_in, dp_in, rw_in, cbias_in,
                  up_in, down_in, sup_in, sdown_in, out):
    BATCH, SEQ, D = x_in.shape
    N = wb_in.shape[0]
    E, _, I = up_in.shape
    SH = sup_in.shape[1]
    T = BATCH * SEQ
    CT = 512
    NCH = T // CT
    CPB = SEQ // CT
    KB = CT // P
    PAIRS = E // 2
    SHP = SH // P
    SLOTS = PAIRS + SHP
    QUARTERS = 4
    G, TOPG = 8, 4
    BUFS = 4
    EG = E // G

    x_flat = x_in.rearrange("b l d -> (b l) d")
    out_flat = out.rearrange("b l d -> (b l) d")

    def x_chunk(c):
        return x_flat[bass.ds(c * CT, CT), :].rearrange("(k p) d -> p k d", p=P)

    def out_chunk(c):
        return out_flat[bass.ds(c * CT, CT), :].rearrange("(k p) d -> p k d", p=P)

    kept = nc.dram_tensor("rest_kept_dram", (P, T), F32).ap()
    bc_dram = nc.dram_tensor("bc_dram", (2 * N, T), F32).ap()

    def col(v):
        return v.rearrange("(p a) -> p a", a=1)

    with ExitStack() as ctx:
        def sb(name, shape, dt=F32):
            return ctx.enter_context(nc.sbuf_tensor(name, shape, dt))

        def sem(name):
            return ctx.enter_context(nc.semaphore(name))

        up_hi, up_lo = sb("up_hi", [P, E * I], F32R), sb("up_lo", [P, E * I], F32R)
        down = sb("down", [P, PAIRS, D])
        sup_hi, sup_lo = sb("sup_hi", [P, SH], F32R), sb("sup_lo", [P, SH], F32R)
        sdown = sb("sdown", [P, SHP, D])
        proj_hi, proj_lo = sb("proj_hi", [P, 3, P], F32R), sb("proj_lo", [P, 3, P], F32R)
        onehot_e = sb("onehot_e", [P, E, I], F32R)
        ident = sb("ident", [P, P])
        a16 = sb("a16", [P, N])
        dtbias, dtmid = sb("dtbias", [P, 1]), sb("dtmid", [P, 1])
        bdt, dp = sb("bdt", [P, 1]), sb("dp", [P, 1])
        keep = sb("keep", [P, NCH])
        cbias = sb("cbias", [P, E])
        halves = sb("halves", [P, KB])
        dt_all, dtx_all = sb("dt_all", [P, T]), sb("dtx_all", [P, T])
        bc_all = sb("bc_all", [2 * N, T])

        x_hi, x_lo = sb("x_hi", [P, 2 * CT], F32R), sb("x_lo", [P, 2 * CT], F32R)
        rest = sb("rest", [P, 2 * CT])
        comb = sb("comb", [P, 2 * CT], F32R)

        xs, xn = sb("xs", [P, KB, D]), sb("xn", [P, KB, D])
        stats, mv = sb("stats", [P, KB, 6]), sb("mv", [P, KB, 2])
        vare, rstd = sb("vare", [P, KB]), sb("rstd", [P, KB])
        xt = sb("xt", [P, CT])
        zt, wexp, poly, zpos = sb("zt", [P, CT]), sb("wexp", [P, CT]), sb("poly", [P, CT]), sb("zpos", [P, CT])
        logit = xn[:, :, :].rearrange("p k d -> p (k d)")
        sig, sfc = sb("sig", [P, KB, E]), sb("sfc", [P, KB, E])
        t4 = sb("t4", [P, 2, KB * G, 4])
        t4a, t4b = t4[:, 0], t4[:, 1]
        t2a, t2b, t2c = sb("t2a", [P, KB * G, 2]), sb("t2b", [P, KB * G, 2]), sb("t2c", [P, KB * G, 2])
        g1a, g1b, g1c = sb("g1a", [P, KB * G]), sb("g1b", [P, KB * G]), sb("g1c", [P, KB * G])
        gtop, top8 = sb("gtop", [P, KB, 8]), sb("top8", [P, KB, 8])
        masked, picked = sb("masked", [P, KB, E]), sb("picked", [P, KB, E])
        sfc_g = sfc[:, :, :].rearrange("p k (g e) -> p (k g) e", g=G)
        wsum, wrec = sb("wsum", [P, KB]), sb("wrec", [P, KB])
        cc = sb("cc", [P, KB, 2, E])

        relu, sq, act = sb("relu", [P, 2, CT]), sb("sq", [P, 2, CT]), sb("act", [P, 3, CT])
        decay = sb("decay", [P, 2, CT])
        b_rows, c_rows = sb("b_rows", [P, BUFS, CT]), sb("c_rows", [P, BUFS, CT])
        h = sb("h", [P, 2, CT])
        carry = sb("carry", [P, N])
        yacc = sb("yacc", [P, CT])
        ot, xr, res = sb("ot", [P, CT]), sb("xr", [P, KB, D]), sb("res", [P, KB, D])
        gmax = sb("gmax", [P, NCH])
        gm1, gmt, flag = sb("gm1", [P, 1]), sb("gmt", [1, 1]), sb("flag", [1, 1], I32)
        colb = sb("colb", [2 * N, 2, P])
        ones = relu[:, 0, 0:P]
        bcs, hs, da = (relu[:, 1, o:o + 2 * w].rearrange("p (b n) -> p b n", b=2)
                       for o, w in ((0, 2 * N), (128, N), (192, N)))
        junk, ss, nrm, scl = sb("junk", [P, 2, N]), sb("ss", [P, 2]), sb("nrm", [P, 2]), sb("scl", [P, 2])

        PARTS = [(0, 1, P), (1, 1, 2 * N), (2, P // E, E)]

        def proj_part(t, k, reps, width):
            return t[:, k, 0:reps * width].rearrange("p (r w) -> p r w", r=reps)

        def transposed(k, reps, width):
            start = (0, P, P + 2 * N)[k]
            return M[:, start:start + width].unsqueeze(1).broadcast_to([P, reps, width])

        QW = E * I // QUARTERS
        up_raw = [dtx_all[:, QW * (q + 1):QW * (q + 2)] for q in range(QUARTERS - 1)] + [dt_all[:, 2 * QW:3 * QW]]
        small = dt_all[:, 0:2 * P].rearrange("p (a k) -> p a k", a=2)
        sup_raw = dt_all[:, 3 * P:3 * P + SH]
        alog = dt_all[:, 1024:1024 + N]
        th = dt_all[:, 1088:1088 + N]
        ea = dt_all[:, 1152:1152 + N]
        oh64 = dtx_all[:, P:P + E]

        def bank(name, banks=1):
            return ctx.enter_context(nc.psum_tensor(name, [P, banks * CT], F32))

        U = [bank("U0"), bank("U1")]
        CB = [bank("CB0"), bank("CB1")]
        DN = bank("DN", 2)
        GR = bank("GR")
        M = bank("M")

        w_small, w_late, w_sdown = sem("w_small"), sem("w_late"), sem("w_sdown")
        w_up = [sem(f"w_up{q}") for q in range(QUARTERS)]
        w_down = [sem(f"w_down{q}") for q in range(QUARTERS)]
        const_ready, pool_init = sem("const_ready"), sem("pool_init")
        wt_ready, proj_ready, up_high, up_split, act_init, dve_init = (
            sem("wt_ready"), sem("proj_ready"), sem("up_high"), sem("up_split"), sem("act_init"), sem("dve_init"))
        x_loaded, xr_loaded, stored = sem("x_loaded"), sem("xr_loaded"), sem("stored")
        dve_prep, pool_prep, act_prep = sem("dve_prep"), sem("pool_prep"), sem("act_prep")
        var_ready, rstd_ready, xn_ready = sem("var_ready"), sem("rstd_ready"), sem("xn_ready")
        xt_done, xhi_ready, xlo_ready = sem("xt_done"), sem("xhi_ready"), sem("xlo_ready")
        z_done, z_copied, sp_ready, th_ready, dt_ready, dtx_ready = (
            sem("z_done"), sem("z_copied"), sem("sp_ready"), sem("th_ready"),
            sem("dt_ready"), sem("dtx_ready"))
        bc_done, bc_ready, bc_stored = sem("bc_done"), sem("bc_ready"), sem("bc_stored")
        lg_done, lg_copied, lgt_done, sig_exp = sem("lg_done"), sem("lg_copied"), sem("lgt_done"), sem("sig_exp")
        poly_added, poly_scaled = sem("poly_added"), sem("poly_scaled")
        sig_one, sig_ready, sfc_ready = sem("sig_one"), sem("sig_ready"), sem("sfc_ready")
        cc_ready, ct_done, chi_ready, clo_ready = sem("cc_ready"), sem("ct_done"), sem("chi_ready"), sem("clo_ready")
        up_done, relu_done, sq_done, cb_done, mul_done, down_done = (
            sem("up_done"), sem("relu_done"), sem("sq_done"), sem("cb_done"), sem("mul_done"), sem("down_done"))
        tanh_done, exp_done, db_done, scan_done = (
            sem("tanh_done"), sem("exp_done"), sem("db_done"), sem("scan_done"))
        ym_done, yacc_done, carry_done, gram_done = (
            sem("ym_done"), sem("yacc_done"), sem("carry_done"), sem("gram_done"))
        sqp_done = sem("sqp_done")
        zpos_ready, rest_begun = sem("zpos_ready"), sem("rest_begun")
        dn_copied, rest_done, rest_kept, s_rest = sem("dn_copied"), sem("rest_done"), sem("rest_kept"), sem("s_rest")
        b_loaded = [sem(f"b_loaded{j}") for j in range(BUFS)]
        c_loaded = [sem(f"c_loaded{j}") for j in range(BUFS)]
        ot_ready, ot_done, res_ready, diag_done, gmax_done = (
            sem("ot_ready"), sem("ot_done"), sem("res_ready"), sem("diag_done"), sem("gmax_done"))
        g_end, flag_ready = sem("g_end"), sem("flag_ready")
        ot_begun = sem("ot_begun")
        passed = sem("passed")
        s_step_dve = sem("s_step_dve")
        s_col, s_bc, s_exp, s_ss, s_norm, s_sqrt, s_ot, s_otd, s_res, s_store, s_xr = (
            sem("s_col"), sem("s_bc"), sem("s_exp"), sem("s_ss"), sem("s_norm"),
            sem("s_sqrt"), sem("s_ot"), sem("s_otd"), sem("s_res"), sem("s_store"), sem("s_xr"))

        def wait(eng, s, value):
            if not isinstance(value, int) or value > 0:
                eng.wait_ge(s, value)

        def alone(eng):
            eng.sem_inc(passed, 1)

        def act_at(slot):
            return act[:, slot % 3, :] if slot < PAIRS else (wexp[:, :] if slot == PAIRS else zt[:, :])

        def sl(c):
            return bass.ds(c * CT, CT)

        def par(c):
            return bass.ds((c % 2) * CT, CT)

        SQ_POOL = [9, 11, 13]
        STEPS = len(LOG1P) - 1
        DVE_PREP = 22
        POOL_PREP = 2

        class Chain:

            def __init__(self, eng, s, base):
                self.eng, self.s, self.base, self.n = eng, s, base, 0

            def then(self, ins):
                ins.then_inc(self.s, 1)
                self.n += 1

            def wait(self, by_itself=False):
                wait(self.eng, self.s, self.base + self.n)
                if by_itself:
                    alone(self.eng)

        def wait_square(eng, c, slot):
            if slot < 0:
                c, slot = c - 1, slot + SLOTS
            on_pool = slot in SQ_POOL
            mine = [k for k in range(SLOTS) if (k in SQ_POOL) == on_pool]
            wait(eng, sqp_done if on_pool else sq_done, c * len(mine) + mine.index(slot) + 1)

        block = ctx.enter_context(nc.Block())

        @block.sync
        def _(sp):
            sp.dma_start(xs[:, :, :], x_chunk(0)).then_inc(x_loaded, 16)
            sp.dma_start(small[:, 0, :], wdt_in).then_inc(w_small, 16)
            sp.dma_start(small[0:N, 1, :], wb_in).then_inc(w_small, 16)
            sp.dma_start(small[N:2 * N, 1, :], wc_in).then_inc(w_small, 16)
            sp.dma_start(small[2 * N:2 * N + E, 1, :], rw_in).then_inc(w_small, 16)
            for q in range(QUARTERS):
                e0, e1 = q * E // QUARTERS, (q + 1) * E // QUARTERS
                sp.dma_start(up_raw[q].rearrange("p (e i) -> p e i", i=I),
                             up_in[e0:e1].rearrange("e h i -> h e i")).then_inc(w_up[q], 16)
                sp.dma_start(down[:, e0 // 2:e1 // 2, :],
                             down_in[e0:e1].rearrange("(j e) i h -> (e i) j h", e=2)).then_inc(w_down[q], 16)
            sp.dma_start(sdown[:, :, :], sdown_in.rearrange("(j p) h -> p j h", p=P)).then_inc(w_sdown, 16)

            def x_in_time(c, first, last):
                if not first:
                    wait(sp, stored, 16 * (c - 1))
                    alone(sp)
                    sp.dma_start(xr[:, :, :], x_chunk(c - 1)).then_inc(xr_loaded, 16)
                if not last:
                    sp.wait_ge(xn_ready, c + 1)
                    alone(sp)
                    sp.dma_start(xs[:, :, :], x_chunk(c + 1)).then_inc(x_loaded, 16)

            def store_rest(c):
                sp.wait_ge(rest_done, c + 1)
                alone(sp)
                sp.dma_start(kept[:, sl(c)], rest[:, par(c)]).then_inc(rest_kept, 16)

            def store_result(c):
                sp.wait_ge(res_ready, c + 1)
                alone(sp)
                sp.dma_start(out_chunk(c), res[:, :, :]).then_inc(stored, 16)

            def rows(c, n, first):
                j = n % BUFS
                if n == 0:
                    sp.wait_ge(bc_ready, c + 1)
                    alone(sp)
                    sp.dma_start(bc_dram[:, sl(c)], bc_all[:, sl(c)]).then_inc(bc_stored, 16)
                    sp.wait_ge(bc_stored, 16 * (c + 1))
                    alone(sp)
                if not first or n >= BUFS:
                    sp.wait_ge(scan_done, c * N + n - BUFS + 1)
                alone(sp)
                sp.dma_start(b_rows[:, j, :], bc_dram[n:n + 1, sl(c)].broadcast_to([P, CT])).then_inc(b_loaded[j], 16)
                if n == BUFS:
                    sp.wait_ge(ym_done, c * N + 1)
                elif not first or n > BUFS:
                    sp.wait_ge(yacc_done, c * (N - 1) + n - BUFS + (1 if n < BUFS else 0))
                alone(sp)
                sp.dma_start(c_rows[:, j, :], bc_dram[N + n:N + n + 1, sl(c)].broadcast_to([P, CT])).then_inc(c_loaded[j], 16)

            def transfers(c, first, last):
                for n in range(N):
                    if n == 0:
                        x_in_time(c, first, last)
                    if n == BUFS + 4 and not first:
                        store_rest(c - 1)
                        store_result(c - 1)
                    rows(c, n, first)

            transfers(0, True, False)
            with sp.Fori(1, NCH - 1) as c:
                transfers(c, False, False)
            transfers(NCH - 1, False, True)
            sp.wait_ge(stored, 16 * (NCH - 1))
            sp.dma_start(xr[:, :, :], x_chunk(NCH - 1)).then_inc(xr_loaded, 16)
            store_result(NCH - 1)
            store_rest(NCH - 1)
            sp.wait_ge(stored, 16 * NCH)
            sp.wait_ge(rest_kept, 16 * NCH)
            sp.wait_ge(flag_ready, 1)
            safe = sp.value_load(flag[0:1, 0:1])
            with sp.If(safe == 0):
                with sp.Fori(0, NCH) as c:
                    sp.dma_start(rest[:, 0:CT], kept[:, sl(c)]).then_inc(s_rest, 16)
                    sp.dma_start(xr[:, :, :], x_chunk(c)).then_inc(s_xr, 16)
                    sp.wait_ge(s_res, c + 1)
                    alone(sp)
                    sp.dma_start(out_chunk(c), res[:, :, :]).then_inc(s_store, 16)
                    sp.wait_ge(s_store, 16 * (c + 1))
                    alone(sp)

        @block.gpsimd
        def _(pool):
            g = nc.gpsimd
            n_init = [0]

            def init(ins):
                ins.then_inc(pool_init, 1)
                n_init[0] += 1
                pool.wait_ge(pool_init, n_init[0])

            init(g.memset(ident[:, :], 0.0))
            init(g.affine_select(out=ident[:, :], in_=ident[:, :], compare_op=ALU.not_equal, fill=1.0,
                                 base=0, pattern=[[-1, P]], channel_multiplier=1))
            init(g.memset(oh64, 0.0))
            for base in (0, -E):
                init(g.affine_select(out=oh64, in_=oh64, compare_op=ALU.not_equal, fill=1.0,
                                     base=base, pattern=[[-1, E]], channel_multiplier=1))
            init(g.memset(halves[:, :], -0.5))
            init(g.memset(keep[:, :], 1.0))
            for b in range(BATCH):
                init(g.memset(keep[:, b * CPB:b * CPB + 1], 0.0))
            init(g.memset(carry[:, :], 0.0))
            g.memset(gmt[:, :], 0.0).then_inc(const_ready, 1)

            def prep(pc, slot):
                chain = chains["p"]
                if slot == 1:
                    pool.wait_ge(var_ready, pc + 1)
                    alone(pool)
                    chain.then(g.tensor_scalar(vare[:, :], mv[:, :, 1], 1e-5, None, ALU.add))
                    chain.wait(True)
                    g.tensor_tensor(rstd[:, :], vare[:, :], halves[:, :], ALU.pow).then_inc(rstd_ready, 1)
                if slot == 7:
                    pool.wait_ge(xlo_ready, pc + 1)
                    pool.wait_ge(xhi_ready, pc + 1)
                    alone(pool)
                    chain.then(g.tensor_tensor(xt[:, :], x_hi[:, par(pc)].bitcast(F32),
                                               x_lo[:, par(pc)].bitcast(F32), ALU.add))
                k, odd = divmod(slot - 11, 2)
                if 0 <= k < STEPS and not odd:
                    pool.wait_ge(poly_added, pc * STEPS + k + 1)
                    g.tensor_tensor(poly[:, :], poly[:, :], wexp[:, :], ALU.mult).then_inc(poly_scaled, 1)
                if slot == 11 + 2 * STEPS:
                    pool.wait_ge(zpos_ready, pc + 1)
                    pool.wait_ge(poly_scaled, (pc + 1) * STEPS)
                    g.tensor_tensor(poly[:, :], poly[:, :], zpos[:, :], ALU.add).then_inc(sp_ready, 1)
                if slot == 17:
                    pool.wait_ge(sig_ready, pc + 1)
                    alone(pool)
                    g.tensor_tensor(sfc[:, :, :], sig[:, :, :], cbias[:, :].unsqueeze(1).broadcast_to([P, KB, E]),
                                    ALU.add).then_inc(sfc_ready, 1)
                if slot == 30:
                    pool.wait_ge(dt_ready, pc + 1)
                    alone(pool)
                    if not isinstance(pc, int) or pc > 1:
                        pool.wait_ge(rest_kept, 16 * (pc - 1))
                        alone(pool)
                    g.tensor_tensor(dtx_all[:, sl(pc)], dt_all[:, sl(pc)], xt[:, :], ALU.mult).then_inc(dtx_ready, 1)
                    g.tensor_tensor(rest[:, par(pc)], xt[:, :], dp[:, 0:1].broadcast_to([P, CT]),
                                    ALU.mult).then_inc(rest_begun, 1)

            def split_up(q):
                cols = slice(q * E * I // QUARTERS, (q + 1) * E * I // QUARTERS)
                pool.wait_ge(up_high, q + 1)
                g.tensor_tensor(up_lo[:, cols], up_raw[q], up_hi[:, cols].bitcast(F32),
                                ALU.subtract).then_inc(up_split, 1)

            def square(c, slot):
                pool.wait_ge(relu_done, c * SLOTS + slot + 1)
                wait(pool, mul_done, c * PAIRS + slot - 1)
                r = relu[:, slot % 2, :]
                g.tensor_tensor(sq[:, slot % 2, :], r, r, ALU.mult).then_inc(sqp_done, 1)

            def out_begin(c):
                wait(pool, yacc_done, (c + 1) * (N - 1))
                pool.wait_ge(rest_begun, c + 1)
                alone(pool)
                g.tensor_tensor(ot[:, :], rest[:, par(c)], yacc[:, :], ALU.add).then_inc(ot_begun, 1)

            def out_end(c, last=False):
                pool.wait_ge(dn_copied, c + 1)
                pool.wait_ge(ot_begun, c + 1)
                alone(pool)
                if not last:
                    g.tensor_tensor(ot[:, :], ot[:, :], zt[:, :], ALU.add).then_inc(ot_ready, 1)
                g.tensor_tensor(rest[:, par(c)], rest[:, par(c)], zt[:, :], ALU.add).then_inc(rest_done, 1)

            def main(c, slot):
                if slot % 2 == 0 and 2 <= slot <= 2 * N:
                    n = slot // 2 - 1
                    pool.wait_ge(scan_done, c * N + n + 1)
                    alone(pool)
                    nxt = NCH - 1 if isinstance(c, int) and c == NCH - 1 else c + 1
                    g.tensor_tensor(carry[:, n:n + 1], h[:, n % 2, CT - 1:CT], keep[:, bass.ds(nxt, 1)],
                                    ALU.mult).then_inc(carry_done, 1)
                    if n:
                        pool.wait_ge(ym_done, c * N + n + 1)
                        wait(pool, yacc_done, c * (N - 1) + n - 1)
                        g.tensor_tensor(yacc[:, :], yacc[:, :], c_rows[:, n % BUFS, :], ALU.add).then_inc(yacc_done, 1)

            chains = {}

            def chunk(c, first, last):
                if not last:
                    chains["p"] = Chain(pool, pool_prep, (c + 1) * POOL_PREP)
                for slot in range(SLOTS):
                    if slot == 0 and not first:
                        out_begin(c - 1)
                    if first and slot in (2, 6, 10):
                        split_up(1 + (slot - 2) // 4)
                    if slot == 3 and not first:
                        out_end(c - 1)
                    main(c, slot)
                    if slot in SQ_POOL:
                        square(c, slot)
                    if not last:
                        prep(c + 1, slot)
                assert last or chains["p"].n == POOL_PREP, chains["p"].n

            chains["p"] = Chain(pool, pool_prep, 0)
            for slot in range(SLOTS):
                if slot == 17:
                    pool.wait_ge(w_late, 5 * 16)
                prep(0, slot)
            chunk(0, True, False)
            with pool.Fori(1, NCH - 1) as c:
                chunk(c, False, False)
            chunk(NCH - 1, False, True)
            out_begin(NCH - 1)
            out_end(NCH - 1, True)

        @block.scalar
        def _(act_e):
            a = nc.scalar
            act_e.dma_start(alog, alog_in).then_inc(w_late, 16)
            act_e.dma_start(sup_raw, sup_in).then_inc(w_late, 16)
            act_e.dma_start(bdt[:, :], col(bdt_in)).then_inc(w_late, 16)
            act_e.dma_start(dp[:, :], col(dp_in)).then_inc(w_late, 16)
            act_e.dma_start(cbias[:, :], cbias_in.rearrange("(a e) -> a e", a=1).broadcast_to([P, E])).then_inc(w_late, 16)

            def constants():
                act_e.wait_ge(w_late, 5 * 16)
                a.activation(th, alog, ACT.Tanh, scale=0.1).then_inc(act_init, 1)
                act_e.wait_ge(act_init, 1)
                a.activation(ea, th, ACT.Exp, scale=10.0).then_inc(act_init, 1)
                a.activation(sup_hi[:, :], sup_raw, ACT.Copy).then_inc(act_init, 1)

            act_e.wait_ge(wt_ready, 2)
            for part in PARTS:
                i = a.activation(proj_part(proj_hi, *part), transposed(*part), ACT.Copy)
            i.then_inc(proj_ready, 1)

            def prep(pc, slot):
                if slot == 6:
                    act_e.wait_ge(xt_done, pc + 1)
                    alone(act_e)
                    a.activation(x_hi[:, par(pc)], M[:, :], ACT.Copy).then_inc(xhi_ready, 1)
                if slot == 11:
                    act_e.wait_ge(lg_done, pc + 1)
                    a.activation(logit[:, :], M[:, :], ACT.Copy).then_inc(lg_copied, 1)
                if slot == 25:
                    a.activation(zpos[:, :], zt[:, :], ACT.Relu).then_inc(zpos_ready, 1)
                if slot == 13:
                    act_e.wait_ge(lgt_done, pc + 1)
                    a.activation(sig[:, :, :].rearrange("p k e -> p (k e)"), M[:, 0:KB * E], ACT.Exp,
                                 scale=-1.0).then_inc(sig_exp, 1)
                    act_e.wait_ge(sig_exp, pc + 1)
                    alone(act_e)
                    a.activation(sig[:, :, :], sig[:, :, :], ACT.Copy, bias=1.0).then_inc(sig_one, 1)
                if slot == 9:
                    act_e.wait_ge(z_done, pc + 1)
                    wait(act_e, sp_ready, pc)
                    if not isinstance(pc, int) or pc > 1:
                        act_e.wait_ge(rest_done, pc - 1)
                    a.activation(zt[:, :], M[:, :], ACT.Identity, bias=bdt[:, 0:1]).then_inc(z_copied, 1)
                    act_e.wait_ge(z_copied, pc + 1)
                    a.activation(wexp[:, :], zt[:, :], ACT.Abs).then_inc(act_prep, 1)
                if slot == 10:
                    act_e.wait_ge(act_prep, 2 * pc + 1)
                    a.activation(wexp[:, :], wexp[:, :], ACT.Exp, scale=-1.0).then_inc(act_prep, 1)
                    act_e.wait_ge(act_prep, 2 * pc + 2)
                    alone(act_e)
                    if not isinstance(pc, int) or pc > 1:
                        act_e.wait_ge(gmax_done, pc - 1)
                    a.activation(poly[:, :], wexp[:, :], ACT.Copy, scale=LOG1P[-1], bias=LOG1P[-2]).then_inc(poly_added, 1)
                k, odd = divmod(slot - 12, 2)
                if 0 <= k < STEPS - 1 and not odd:
                    act_e.wait_ge(poly_scaled, pc * STEPS + k + 1)
                    a.activation(poly[:, :], poly[:, :], ACT.Copy, bias=LOG1P[STEPS - 2 - k]).then_inc(poly_added, 1)
                if slot == 16:
                    act_e.wait_ge(bc_done, pc + 1)
                    alone(act_e)
                    a.activation(bc_all[:, sl(pc)], M[0:2 * N, :], ACT.Copy).then_inc(bc_ready, 1)
                if slot == 28:
                    act_e.wait_ge(sp_ready, pc + 1)
                    a.activation(zt[:, :], poly[:, :], ACT.Tanh, scale=0.5 / DT_HALF,
                                 bias=dtbias[:, 0:1]).then_inc(th_ready, 1)
                if slot == 29:
                    act_e.wait_ge(th_ready, pc + 1)
                    alone(act_e)
                    a.activation(dt_all[:, sl(pc)], zt[:, :], ACT.Identity, scale=2.0 * DT_HALF,
                                 bias=dtmid[:, 0:1]).then_inc(dt_ready, 1)
                if slot == 32:
                    act_e.wait_ge(ct_done, pc + 1)
                    alone(act_e)
                    a.activation(comb[:, par(pc)], M[:, :], ACT.Copy).then_inc(chi_ready, 1)

            def main(c, slot):
                s = c * SLOTS + slot
                n = slot // 2
                act_e.wait_ge(up_done, s + 1)
                wait_square(act_e, c, slot - 2)
                a.activation(relu[:, slot % 2, :], U[slot % 2][:, :], ACT.Relu).then_inc(relu_done, 1)
                if n < N and slot % 2 == 0:
                    wait(act_e, scan_done, c * N + n - 1)
                    alone(act_e)
                    a.activation(decay[:, n % 2, :], dt_all[:, sl(c)], ACT.Tanh, scale=a16[:, n:n + 1]).then_inc(tanh_done, 1)
                if n < N and slot % 2 == 1:
                    act_e.wait_ge(tanh_done, c * N + n + 1)
                    a.activation(decay[:, n % 2, :], decay[:, n % 2, :], ACT.Exp, scale=16.0).then_inc(exp_done, 1)
                if slot in SQ_POOL:
                    return
                act_e.wait_ge(relu_done, s + 1)
                if slot < PAIRS:
                    wait(act_e, mul_done, c * PAIRS + slot - 1)
                    dst = sq[:, slot % 2, :]
                else:
                    dst = act_at(slot)
                a.activation(dst, relu[:, slot % 2, :], ACT.Square).then_inc(sq_done, 1)

            def dn_copy(c):
                act_e.wait_ge(down_done, (c + 1) * SLOTS)
                a.activation(zt[:, :], DN[:, par(c)], ACT.Copy).then_inc(dn_copied, 1)

            def split_up(q):
                cols = slice(q * E * I // QUARTERS, (q + 1) * E * I // QUARTERS)
                act_e.wait_ge(w_up[q], 16)
                a.activation(up_hi[:, cols], up_raw[q], ACT.Copy).then_inc(up_high, 1)

            def chunk(c, first, last):
                for slot in range(SLOTS):
                    if slot == 3 and not first:
                        dn_copy(c - 1)
                    if slot == 0:
                        act_e.wait_ge(dt_ready, c + 1)
                    main(c, slot)
                    if not last:
                        prep(c + 1, slot)

            for slot in range(SLOTS):
                if slot == 7:
                    constants()
                if slot in (12, 18, 22, 26):
                    split_up((12, 18, 22, 26).index(slot))
                if slot == 28:
                    act_e.wait_ge(dve_init, 4)
                prep(0, slot)
            chunk(0, True, False)
            with act_e.Fori(1, NCH - 1) as c:
                chunk(c, False, False)
            chunk(NCH - 1, False, True)
            act_e.wait_ge(ot_ready, NCH)
            dn_copy(NCH - 1)

            act_e.wait_ge(flag_ready, 1)
            safe = act_e.value_load(flag[0:1, 0:1])
            with act_e.If(safe == 0):
                with act_e.Fori(0, SEQ) as t:
                    for b in range(2):
                        i = a.activation(da[:, b, :], a16[:, :], ACT.Tanh, scale=dt_all[:, bass.ds(t + b * SEQ, 1)])
                    i.then_inc(s_exp, 1)
                    act_e.wait_ge(s_exp, 2 * t + 1)
                    a.activation(da[:, :, :], da[:, :, :], ACT.Exp, scale=16.0).then_inc(s_exp, 1)
                    act_e.wait_ge(s_norm, t + 1)
                    a.activation(nrm[:, :], M[:, 64:66], ACT.Sqrt).then_inc(s_sqrt, 1)

        @block.vector
        def _(dve):
            v = nc.vector
            v.memset(dtbias[:, :], -0.5 * DT_MID / DT_HALF).then_inc(dve_init, 1)
            v.memset(dtmid[:, :], DT_MID).then_inc(dve_init, 1)
            dve.wait_ge(const_ready, 1)

            def constants(slot):
                if slot == 3:
                    dve.wait_ge(proj_ready, 1)
                    for part in PARTS:
                        i = v.tensor_tensor(proj_part(proj_lo, *part), transposed(*part),
                                            proj_part(proj_hi.bitcast(F32), *part), ALU.subtract)
                    i.then_inc(proj_ready, 1)
                if slot == 8:
                    dve.wait_ge(act_init, 3)
                    v.tensor_scalar(a16[:, :], ea, -1.0 / 16, None, ALU.mult).then_inc(dve_init, 1)
                    v.tensor_tensor(sup_lo[:, :], sup_raw, sup_hi[:, :].bitcast(F32), ALU.subtract)
                if slot == 12:
                    dve.wait_ge(up_high, 1)
                    split = slice(0, E * I // QUARTERS)
                    v.tensor_tensor(up_lo[:, split], up_raw[0], up_hi[:, split].bitcast(F32),
                                    ALU.subtract).then_inc(up_split, 1)
                if slot == 7:
                    v.tensor_copy(onehot_e[:, :, :], oh64.unsqueeze(2).broadcast_to([P, E, I])).then_inc(dve_init, 1)

            def dup(t, n):
                return t.unsqueeze(2).broadcast_to([P, KB * G, n])

            RECIP_AT = {14: [0], 15: [1, 2], 16: [3]}

            def prep(pc, slot):
                ch = chains["v"]

                def op(f, *args, **kw):
                    ch.wait(f in (v.max, v.match_replace))
                    ch.then(f(*args, **kw))

                if slot == -0.5:
                    dve.wait_ge(x_loaded, 16 * (pc + 1))
                    for k in range(KB):
                        i = v.bn_stats(stats[:, k, :], xs[:, k, :])
                    ch.then(i)
                    ch.wait(True)
                    for k in range(KB):
                        i = v.bn_aggr(mv[:, k, :], stats[:, k, :])
                    i.then_inc(var_ready, 1)
                if slot == 3:
                    dve.wait_ge(rstd_ready, pc + 1)
                    wait(dve, lgt_done, pc)
                    for k in range(KB):
                        i = v.tensor_scalar(xn[:, k, :], xs[:, k, :], mv[:, k, 0:1], rstd[:, k:k + 1],
                                            ALU.subtract, ALU.mult)
                    i.then_inc(xn_ready, 1)
                if slot == 7:
                    dve.wait_ge(xhi_ready, pc + 1)
                    v.tensor_tensor(x_lo[:, par(pc)], M[:, :], x_hi[:, par(pc)].bitcast(F32),
                                    ALU.subtract).then_inc(xlo_ready, 1)
                for k in RECIP_AT.get(slot, []):
                    if k == 0:
                        dve.wait_ge(sig_one, pc + 1)
                    i = v.reciprocal(sig[:, k, :], sig[:, k, :])
                    if k == KB - 1:
                        i.then_inc(sig_ready, 1)
                if slot == 18:
                    dve.wait_ge(sfc_ready, pc + 1)
                    v.tensor_tensor(t4a[:, :, :], sfc_g[:, :, 0:4], sfc_g[:, :, 4:8], ALU.max)
                    ch.then(v.tensor_tensor(t4b[:, :, :], sfc_g[:, :, 0:4], sfc_g[:, :, 4:8], ALU.min))
                if slot == 18.5:
                    ch.wait()
                    v.tensor_tensor(t2a[:, :, :], t4a[:, :, 0:2], t4a[:, :, 2:4], ALU.max)
                    v.tensor_tensor(t2b[:, :, :], t4a[:, :, 0:2], t4a[:, :, 2:4], ALU.min)
                    ch.then(v.tensor_tensor(t2c[:, :, :], t4b[:, :, 0:2], t4b[:, :, 2:4], ALU.max))
                if slot == 19:
                    op(v.tensor_tensor, t2b[:, :, :], t2b[:, :, :], t2c[:, :, :], ALU.max)
                if slot == 19.5:
                    ch.wait()
                    v.tensor_tensor(g1a[:, :], t2a[:, :, 0], t2a[:, :, 1], ALU.max)
                    v.tensor_tensor(g1b[:, :], t2a[:, :, 0], t2a[:, :, 1], ALU.min)
                    ch.then(v.tensor_tensor(g1c[:, :], t2b[:, :, 0], t2b[:, :, 1], ALU.max))
                if slot == 20:
                    op(v.tensor_tensor, g1b[:, :], g1b[:, :], g1c[:, :], ALU.max)
                if slot == 20.5:
                    op(v.tensor_tensor, g1a[:, :], g1a[:, :], g1b[:, :], ALU.add)
                if slot == 21:
                    ch.wait(True)
                    for k in range(KB):
                        i = v.max(gtop[:, k, :], g1a[:, k * G:(k + 1) * G])
                    ch.then(i)
                if slot == 21.5:
                    op(v.memset, gtop[:, :, TOPG:], 3.0e38)
                if slot == 22:
                    ch.wait(True)
                    for k in range(KB):
                        groups = slice(k * G, (k + 1) * G)
                        i = v.match_replace(out=g1b[:, groups], in_to_replace=gtop[:, k, :],
                                            in_values=g1a[:, groups], imm_value=-3.0e38)
                    ch.then(i)
                if slot == 22.5:
                    op(v.tensor_tensor, g1c[:, :], g1a[:, :], g1b[:, :], ALU.not_equal)
                if slot == 23:
                    op(v.tensor_tensor, masked[:, :, :].rearrange("p k (g e) -> p (k g) e", g=G), sfc_g,
                       dup(g1c[:, :], EG), ALU.mult)
                if slot == 23.5:
                    op(v.tensor_scalar, masked[:, :, :], masked[:, :, :], 0.0, None, ALU.add)
                if slot in (24, 25):
                    ch.wait(True)
                    for k in range(KB // 2) if slot == 24 else range(KB // 2, KB):
                        i = v.max(top8[:, k, :], masked[:, k, :])
                    ch.then(i)
                if slot in (25.5, 26.5):
                    ch.wait(True)
                    for k in range(KB // 2) if slot == 25.5 else range(KB // 2, KB):
                        i = v.match_replace(out=picked[:, k, :], in_to_replace=top8[:, k, :],
                                            in_values=masked[:, k, :], imm_value=-3.0e38)
                    ch.then(i)
                if slot == 27:
                    op(v.tensor_tensor, picked[:, :, :], picked[:, :, :], masked[:, :, :], ALU.not_equal)
                if slot == 27.5:
                    op(v.tensor_tensor, picked[:, :, :], picked[:, :, :], sig[:, :, :], ALU.mult)
                if slot == 28.5:
                    op(v.tensor_reduce, wsum[:, :], picked[:, :, :], axis=AX.X, op=ALU.add)
                if slot == 29:
                    op(v.tensor_scalar, wsum[:, :], wsum[:, :], 1e-20, 1 / 2.5, ALU.add, ALU.mult)
                if slot == 29.5:
                    op(v.reciprocal, wrec[:, :], wsum[:, :])
                if slot == 30.5:
                    ch.wait()
                    wait(dve, ct_done, pc)
                    for r in range(2):
                        i = v.tensor_tensor(cc[:, :, r, :], picked[:, :, :],
                                            wrec[:, :].unsqueeze(2).broadcast_to([P, KB, E]), ALU.mult)
                    i.then_inc(cc_ready, 1)
                if slot == 33:
                    dve.wait_ge(chi_ready, pc + 1)
                    v.tensor_tensor(comb[E:P, par(pc)], M[E:P, :], comb[E:P, par(pc)].bitcast(F32),
                                    ALU.subtract).then_inc(clo_ready, 1)

            def mul(c, slot):
                s = c * SLOTS + slot
                m = c * PAIRS + slot
                wait_square(dve, c, slot)
                dve.wait_ge(cb_done, m + 1)
                wait(dve, down_done, s - 2)
                v.tensor_tensor(act_at(slot), sq[:, slot % 2, :], CB[slot % 2][:, :], ALU.mult).then_inc(mul_done, 1)

            def ymul(c, n):
                dve.wait_ge(scan_done, c * N + n + 1)
                dve.wait_ge(c_loaded[n % BUFS], 16 * (c * (N // BUFS) + n // BUFS + 1))
                if n == 0:
                    wait(dve, ot_begun, c)
                dst = c_rows[:, n % BUFS, :] if n else yacc[:, :]
                v.tensor_tensor(dst, h[:, n % 2, :], c_rows[:, n % BUFS, :], ALU.mult).then_inc(ym_done, 1)

            diag = poly[:, :].rearrange("p (k t) -> p k t", k=KB)

            def norms(c, part):
                if part == 0:
                    dve.wait_ge(gram_done, (c + 1) * N)
                    v.tensor_tensor(diag, GR[:, :].rearrange("p (k t) -> p k t", k=KB),
                                    ident[:, :].unsqueeze(1).broadcast_to([P, KB, P]), ALU.mult).then_inc(diag_done, 1)
                else:
                    dve.wait_ge(diag_done, c + 1)
                    v.tensor_reduce(gmax[:, bass.ds(c, 1)], diag, axis=AX.XY, op=ALU.max).then_inc(gmax_done, 1)

            def result(c):
                dve.wait_ge(ot_done, c + 1)
                dve.wait_ge(xr_loaded, 16 * (c + 1))
                v.tensor_tensor(res[:, :, :], M[:, :].rearrange("p (k d) -> p k d", k=KB), xr[:, :, :],
                                ALU.add).then_inc(res_ready, 1)

            chains = {}

            def chunk(c, first, last):
                if not last:
                    chains["v"] = Chain(dve, dve_prep, (c + 1) * DVE_PREP)
                for slot in range(SLOTS):
                    n = slot // 2
                    if slot == 0:
                        dve.wait_ge(dtx_ready, c + 1)
                    if 1 <= slot <= PAIRS:
                        mul(c, slot - 1)
                    if slot % 2 == 0 and 1 <= n <= N:
                        ymul(c, n - 1)
                    if slot == 0 and not first:
                        norms(c - 1, 0)
                    if not last:
                        prep(c + 1, slot - 0.5)
                    if slot == 5 and not first:
                        result(c - 1)
                    if slot % 2 == 0 and n < N:
                        b = b_rows[:, n % BUFS, :]
                        dve.wait_ge(b_loaded[n % BUFS], 16 * (c * (N // BUFS) + n // BUFS + 1))
                        v.tensor_tensor(b, dtx_all[:, sl(c)], b, ALU.mult).then_inc(db_done, 1)
                    if slot == 9 and not first:
                        norms(c - 1, 1)
                    if slot % 2 == 1 and n < N:
                        dve.wait_ge(db_done, c * N + n + 1)
                        dve.wait_ge(exp_done, c * N + n + 1)
                        wait(dve, gram_done, c * N + n - 1)
                        wait(dve, carry_done, c * N + max(n - 1, 0))
                        initial = 0.0 if first else carry[:, n:n + 1]
                        v.tensor_tensor_scan(h[:, n % 2, :], decay[:, n % 2, :], b_rows[:, n % BUFS, :], initial,
                                             ALU.mult, ALU.add).then_inc(scan_done, 1)
                    if not last:
                        prep(c + 1, slot)
                assert last or chains["v"].n == DVE_PREP, chains["v"].n

            chains["v"] = Chain(dve, dve_prep, 0)
            for slot in range(SLOTS):
                prep(0, slot - 0.5)
                prep(0, slot)
                constants(slot)
            chunk(0, True, False)
            with dve.Fori(1, NCH - 1) as c:
                chunk(c, False, False)
            chunk(NCH - 1, False, True)
            norms(NCH - 1, 0)
            norms(NCH - 1, 1)
            dve.wait_ge(down_done, NCH * SLOTS)
            dve.wait_ge(ot_begun, NCH)
            v.tensor_tensor(ot[:, :], ot[:, :], DN[:, par(NCH - 1)], ALU.add).then_inc(ot_ready, 1)
            result(NCH - 1)
            dve.wait_ge(gmax_done, NCH)
            v.tensor_reduce(gm1[:, :], gmax[:, :], axis=AX.X, op=ALU.max).then_inc(g_end, 1)
            dve.wait_ge(g_end, 2)
            v.tensor_reduce(gmt[:, :], GR[0:1, 0:P], axis=AX.X, op=ALU.max).then_inc(g_end, 1)
            dve.wait_ge(g_end, 3)
            v.tensor_scalar(flag[:, :], gmt[:, :], SAFE_SQUARE, None, ALU.is_lt).then_inc(flag_ready, 1)
            dve.wait_ge(flag_ready, 1)
            safe = dve.value_load(flag[0:1, 0:1])
            with dve.If(safe == 0):
                v.memset(ones[:, :], 1.0)
                v.memset(hs[:, :, :], 0.0).then_inc(s_step_dve, 1)
                STEP = 11
                with dve.Fori(0, SEQ) as t:
                    cnt = [0]

                    def link(ins):
                        ins.then_inc(s_step_dve, 1)
                        cnt[0] += 1

                    def linked():
                        dve.wait_ge(s_step_dve, t * STEP + cnt[0] + 1)

                    linked()
                    for b in range(2):
                        i = v.tensor_copy(colb[:, b, :], bc_all[:, bass.ds(t + b * SEQ, 1)].broadcast_to([2 * N, P]))
                    i.then_inc(s_col, 1)
                    dve.wait_ge(s_exp, 2 * t + 2)
                    link(v.tensor_tensor(hs[:, :, :], hs[:, :, :], da[:, :, :], ALU.mult))
                    dve.wait_ge(s_bc, t + 1)
                    link(v.tensor_copy(bcs[:, :, :], M[:, 0:4 * N].rearrange("p (b n) -> p b n", b=2)))
                    linked()
                    for b in range(2):
                        link(v.scalar_tensor_tensor(out=hs[:, b, :], in0=bcs[:, b, 0:N], scalar=dtx_all[:, bass.ds(t + b * SEQ, 1)],
                                                    in1=hs[:, b, :], op0=ALU.mult, op1=ALU.add))
                    linked()
                    for b in range(2):
                        i = v.scalar_tensor_tensor(out=junk[:, b, :], in0=hs[:, b, :], scalar=1.0, in1=hs[:, b, :],
                                                   op0=ALU.mult, op1=ALU.mult, accum_out=ss[:, b:b + 1])
                    i.then_inc(s_ss, 1)
                    dve.wait_ge(s_sqrt, t + 1)
                    link(v.tensor_scalar(nrm[:, :], nrm[:, :], 1e-8, None, ALU.add))
                    linked()
                    link(v.reciprocal(scl[:, :], nrm[:, :]))
                    linked()
                    link(v.tensor_scalar(scl[:, :], scl[:, :], NORM_LIMIT, 1.0, ALU.mult, ALU.min))
                    linked()
                    for b in range(2):
                        link(v.tensor_scalar(hs[:, b, :], hs[:, b, :], scl[:, b:b + 1], None, ALU.mult))
                    linked()
                    for b in range(2):
                        link(v.scalar_tensor_tensor(out=junk[:, b, :], in0=hs[:, b, :], scalar=1.0, in1=bcs[:, b, N:2 * N],
                                                    op0=ALU.mult, op1=ALU.mult, accum_out=ss[:, b:b + 1]))
                    linked()
                    for b in range(2):
                        i = v.tensor_copy(dt_all[:, bass.ds(t + b * SEQ, 1)], ss[:, b:b + 1])
                    assert cnt[0] == STEP, cnt[0]
                with dve.Fori(0, NCH) as c:
                    dve.wait_ge(s_rest, 16 * (c + 1))
                    v.tensor_tensor(ot[:, :], rest[:, 0:CT], dt_all[:, sl(c)], ALU.add).then_inc(s_ot, 1)
                    dve.wait_ge(s_otd, c + 1)
                    dve.wait_ge(s_xr, 16 * (c + 1))
                    v.tensor_tensor(res[:, :, :], M[:, :].rearrange("p (k d) -> p k d", k=KB), xr[:, :, :],
                                    ALU.add).then_inc(s_res, 1)

        @block.tensor
        def _(pe):
            mm = nc.tensor.matmul

            def three(dst, hi, lo, cols, start=True, stop=True):
                mm(dst, hi, x_hi[:, cols], start=start, stop=False)
                mm(dst, hi, x_lo[:, cols], start=False, stop=False)
                return mm(dst, lo, x_hi[:, cols], start=False, stop=stop)

            def transposes(src):
                for k in range(KB):
                    i = nc.tensor.transpose(M[:, k * P:(k + 1) * P], src(k), ident[:, :])
                return i

            pe.wait_ge(const_ready, 1)
            pe.wait_ge(w_small, 16 * 4)
            nc.tensor.transpose(M[:, 0:P], small[:, 0, :], ident[:, :]).then_inc(wt_ready, 1)
            rows = 2 * N + E
            nc.tensor.transpose(M[:, P:P + rows], small[0:rows, 1, :], ident[0:rows, 0:rows]).then_inc(wt_ready, 1)

            def prep(pc, slot):
                if slot == 6:
                    pe.wait_ge(xn_ready, pc + 1)
                    if not isinstance(pc, int) or pc > 1:
                        pe.wait_ge(res_ready, pc - 1)
                    transposes(lambda k: xn[:, k, :]).then_inc(xt_done, 1)
                if slot == 8:
                    pe.wait_ge(xlo_ready, pc + 1)
                    three(M[:, :], proj_hi[:, 0, :], proj_lo[:, 0, :], par(pc)).then_inc(z_done, 1)
                if slot == 10:
                    pe.wait_ge(z_copied, pc + 1)
                    three(M[:, :], proj_hi[:, 2, :], proj_lo[:, 2, :], par(pc)).then_inc(lg_done, 1)
                if slot == 12:
                    pe.wait_ge(lg_copied, pc + 1)
                    alone(pe)
                    for k in range(KB):
                        i = nc.tensor.transpose(M[:, k * E:(k + 1) * E], logit[0:E, k * P:(k + 1) * P], ident[0:E, 0:E])
                    i.then_inc(lgt_done, 1)
                if slot == 15:
                    pe.wait_ge(sig_exp, pc + 1)
                    alone(pe)
                    three(M[0:2 * N, :], proj_hi[:, 1, 0:2 * N], proj_lo[:, 1, 0:2 * N], par(pc)).then_inc(bc_done, 1)
                if slot == 32:
                    pe.wait_ge(cc_ready, pc + 1)
                    pe.wait_ge(bc_ready, pc + 1)
                    transposes(lambda k: cc[:, k, :, :].rearrange("p r e -> p (r e)")).then_inc(ct_done, 1)

            def down_mm(c, slot):
                s = c * SLOTS + slot
                if slot < PAIRS:
                    pe.wait_ge(mul_done, c * PAIRS + slot + 1)
                    w, a = down[:, slot, :], act_at(slot)
                else:
                    wait_square(pe, c, slot)
                    w, a = sdown[:, slot - PAIRS, :], act_at(slot)
                mm(DN[:, par(c)], w, a, start=slot == 0, stop=slot == SLOTS - 1).then_inc(down_done, 1)

            def cb_mm(c, slot):
                wait(pe, mul_done, c * PAIRS + slot - 1)
                mm(CB[slot % 2][:, :], onehot_e[:, 2 * slot:2 * slot + 2, :].rearrange("p e i -> p (e i)"),
                   comb[:, par(c)], start=True, stop=True).then_inc(cb_done, 1)

            def gram(c, n):
                pe.wait_ge(scan_done, c * N + n + 1)
                if n == 0:
                    wait(pe, diag_done, c)
                pe.wait_ge(ym_done, c * N + n + 1)
                top = h[:, n % 2, :].bitcast(BF16).rearrange("p (t two) -> p t two", two=2)
                for k in range(KB):
                    hb = top[:, k * P:(k + 1) * P, 1]
                    i = mm(GR[:, k * P:(k + 1) * P], hb, hb, start=n == 0 and k == 0,
                           stop=n == N - 1 and k == KB - 1, skip_group_check=True)
                i.then_inc(gram_done, 1)

            def chunk(c, first, last):
                for slot in range(SLOTS):
                    s = c * SLOTS + slot
                    n = slot // 2
                    if slot == 0:
                        pe.wait_ge(xlo_ready, c + 1)
                    if first and slot % (PAIRS // QUARTERS) == 0 and slot < PAIRS:
                        pe.wait_ge(up_split, slot // (PAIRS // QUARTERS) + 1)
                    wait(pe, relu_done, s - 1)
                    w = slice(slot * P, (slot + 1) * P)
                    if slot < PAIRS:
                        three(U[slot % 2][:, :], up_hi[:, w], up_lo[:, w], par(c)).then_inc(up_done, 1)
                    else:
                        w = slice((slot - PAIRS) * P, (slot - PAIRS + 1) * P)
                        three(U[slot % 2][:, :], sup_hi[:, w], sup_lo[:, w], par(c)).then_inc(up_done, 1)
                    if 1 <= slot <= PAIRS:
                        if slot == 1:
                            pe.wait_ge(clo_ready, c + 1)
                        cb_mm(c, slot - 1)
                    if 3 < slot:
                        if first and (slot - 3) % (PAIRS // QUARTERS) == 0 and slot - 3 < PAIRS:
                            pe.wait_ge(w_down[(slot - 3) // (PAIRS // QUARTERS)], 16)
                        down_mm(c, slot - 3)
                    elif slot < 3 and not first:
                        down_mm(c - 1, SLOTS - 3 + slot)
                    if slot % 2 == 1 and 1 <= n <= N:
                        gram(c, n - 1)
                    if slot == 3:
                        if first:
                            pe.wait_ge(w_down[0], 16)
                        down_mm(c, 0)
                    if slot == 5 and not first:
                        out_mm(c - 1)
                    if not last:
                        prep(c + 1, slot)

            def out_mm(c):
                pe.wait_ge(ot_ready, c + 1)
                if isinstance(c, int) and c == NCH - 1:
                    pe.wait_ge(res_ready, c)
                else:
                    pe.wait_ge(clo_ready, c + 2)
                transposes(lambda k: ot[:, k * P:(k + 1) * P]).then_inc(ot_done, 1)

            pe.wait_ge(proj_ready, 2)
            for slot in range(SLOTS):
                prep(0, slot)
            pe.wait_ge(dve_init, 4)
            pe.wait_ge(w_sdown, 16)
            chunk(0, True, False)
            with pe.Fori(1, NCH - 1) as c:
                chunk(c, False, False)
            chunk(NCH - 1, False, True)
            for slot in (3, 2, 1):
                down_mm(NCH - 1, SLOTS - slot)
            out_mm(NCH - 1)
            pe.wait_ge(g_end, 1)
            mm(GR[0:1, 0:P], gm1[:, 0:1], ident[:, :], start=True, stop=True).then_inc(g_end, 1)

            pe.wait_ge(flag_ready, 1)
            pe.wait_ge(res_ready, NCH)
            safe = pe.value_load(flag[0:1, 0:1])
            with pe.If(safe == 0):
                with pe.Fori(0, SEQ) as t:
                    pe.wait_ge(s_col, t + 1)
                    for b in range(2):
                        i = mm(M[:, 2 * N * b:2 * N * (b + 1)], colb[:, b, :], ident[0:2 * N, 0:2 * N], start=True, stop=True)
                    i.then_inc(s_bc, 1)
                    pe.wait_ge(s_ss, t + 1)
                    mm(M[:, 64:66], ones[:, :], ss[:, :], start=True, stop=True).then_inc(s_norm, 1)
                with pe.Fori(0, NCH) as c:
                    pe.wait_ge(s_ot, c + 1)
                    transposes(lambda k: ot[:, k * P:(k + 1) * P]).then_inc(s_otd, 1)


_INS = ['L0_attn_x', 'L0_attn_Wdt', 'L0_attn_bdt', 'L0_attn_WB', 'L0_attn_WC', 'L0_attn_A_log', 'L0_attn_Dp',
        'L0_ffn_router_w', 'L0_ffn_correction_bias', 'L0_ffn_up_w', 'L0_ffn_down_w', 'L0_ffn_shared_up_w',
        'L0_ffn_shared_down_w']


def kernel(**inputs):
    import concourse.bacc as _bacc
    from concourse.bass_utils import run_bass_kernel_spmd as _run

    nc = _bacc.Bacc("TRN2", target_bir_lowering=False, num_devices=1)
    arrays, args = {}, []
    for name in _INS:
        a = np.ascontiguousarray(inputs[name])
        arrays[f"in_{name}"] = a
        args.append(nc.dram_tensor(f"in_{name}", a.shape, mybir.dt.from_np(a.dtype), kind="ExternalInput").ap())
    out = nc.dram_tensor("out_0", arrays["in_L0_attn_x"].shape, F32, kind="ExternalOutput").ap()
    layer_program(nc, *args, out)
    r = _run(nc, [arrays], core_ids=[0])
    return r.results[0]["out_0"]
```
